# Optimizing a Trainium2 kernel written in Bass

```python
import numpy as np
import jax
import jax.numpy as jnp

def _softmax(x, axis=-1):
    return jax.nn.softmax(x, axis=axis)

def _gelu(x):
    return jax.nn.gelu(x, approximate=True)

def _silu(x):
    return jax.nn.silu(x)

def _sigmoid(x):
    return jax.nn.sigmoid(x)

def _layernorm(x, axis=-1, eps=1e-05):
    m = jnp.mean(x, axis=axis, keepdims=True)
    v = jnp.var(x, axis=axis, keepdims=True)
    return (x - m) / jnp.sqrt(v + eps)

def _scatter_add(tgt, idx, src, axis=0):
    return tgt.at[idx].add(src)

def _segment_sum(src, seg, n):
    return jax.ops.segment_sum(src, seg, n)
kernel_name = 'mk_metaformer_d1_conv_nchw512_r4_11ce72'

def setup_inputs(seed: int=0):
    np.random.seed(seed)
    _w = jnp.asarray

    def _rec_inputs():
        import jax
        import jax.numpy as jnp
        _gk = jax.random.key(seed)
        x = 7.22e-05 + 1 * jax.random.normal(jax.random.fold_in(_gk, 1), (4, 128, 16, 16), jnp.float32)
        return x
    x = _rec_inputs()

    def _L0_conv_setup():
        import jax, jax.numpy as jnp
        import numpy as np
        N_HEADS = 8
        EPS = 1e-05
        key = jax.random.key(seed)
        ks = jax.random.split(key, 5)
        B, C, H, W = (4, 128, 16, 16)
        X = jax.random.normal(ks[0], (B, C, H, W), dtype=jnp.float32)
        gamma = jnp.ones((C,), dtype=jnp.float32)
        beta = jnp.zeros((C,), dtype=jnp.float32)
        Wqkv = jax.random.normal(ks[1], (3 * C, C), dtype=jnp.float32) * 0.02
        bqkv = jnp.zeros((3 * C,), dtype=jnp.float32)
        Wproj = jax.random.normal(ks[2], (C, C), dtype=jnp.float32) * 0.02
        bproj = jnp.zeros((C,), dtype=jnp.float32)
        return {'X': X, 'gamma': gamma, 'beta': beta, 'Wqkv': Wqkv, 'bqkv': bqkv, 'Wproj': Wproj, 'bproj': bproj}
    _L0_conv_all = _L0_conv_setup()
    _L0_conv_in = {k: v for k, v in _L0_conv_all.items() if k in ('gamma', 'beta', 'Wqkv', 'bqkv', 'Wproj', 'bproj')}
    del _L0_conv_all

    def _L0_ffn_setup():
        import jax, jax.numpy as jnp
        import numpy as np
        BLOCK = 16
        NF4_TABLE = jnp.array([-1.0, -0.6961928009986877, -0.5250730514526367, -0.39491748809814453, -0.28444138169288635, -0.18477343022823334, -0.09105003625154495, 0.0, 0.07958029955625534, 0.16093020141124725, 0.24611230194568634, 0.33791524171829224, 0.44070982933044434, 0.5626170039176941, 0.7229568362236023, 1.0], dtype=jnp.float32)

        def _dequant_nf4(qidx, scales):
            w = NF4_TABLE[qidx].reshape(-1, BLOCK) * scales[:, None]
            return w.reshape(qidx.shape)
        key = jax.random.key(seed)
        k1, k2, k3, k4 = jax.random.split(key, 4)
        x = jax.random.normal(k1, (4, 2048, 128), dtype=jnp.float32)
        qidx = jax.random.randint(k2, (128, 128), 0, 16, dtype=jnp.int32)
        scales = jax.random.uniform(k3, (1024,), dtype=jnp.float32)
        W = jax.random.normal(k4, (128, 128), dtype=jnp.float32) * (1.0 / np.sqrt(512.0))
        return {'x': x, 'qidx': qidx, 'scales': scales, 'W': W}
    _L0_ffn_all = _L0_ffn_setup()
    _L0_ffn_in = {k: v for k, v in _L0_ffn_all.items() if k in ('qidx', 'scales', 'W')}
    del _L0_ffn_all
    return {'x': x, 'L0_conv_gamma': _L0_conv_in['gamma'], 'L0_conv_beta': _L0_conv_in['beta'], 'L0_conv_Wqkv': _L0_conv_in['Wqkv'], 'L0_conv_bqkv': _L0_conv_in['bqkv'], 'L0_conv_Wproj': _L0_conv_in['Wproj'], 'L0_conv_bproj': _L0_conv_in['bproj'], 'L0_ffn_qidx': _L0_ffn_in['qidx'], 'L0_ffn_scales': _L0_ffn_in['scales'], 'L0_ffn_W': _L0_ffn_in['W']}

def reference(x, L0_conv_gamma, L0_conv_beta, L0_conv_Wqkv, L0_conv_bqkv, L0_conv_Wproj, L0_conv_bproj, L0_ffn_qidx, L0_ffn_scales, L0_ffn_W):
    import jax
    import jax.numpy as jnp

    def _L0_conv_ref(X, gamma, beta, Wqkv, bqkv, Wproj, bproj):
        import jax, jax.numpy as jnp
        import numpy as np
        N_HEADS = 8
        EPS = 1e-05
        B, C, H, W = X.shape
        hw = H * W
        d3 = 3 * C // N_HEADS
        scale = jnp.sqrt(jnp.asarray(C / N_HEADS, dtype=X.dtype))
        t = X.reshape(B, C, hw).transpose(0, 2, 1)
        mu = jnp.mean(t, axis=-1, keepdims=True)
        var = jnp.var(t, axis=-1, keepdims=True)
        t = (t - mu) * jax.lax.rsqrt(var + EPS) * gamma + beta
        t = t @ Wqkv.T + bqkv
        t = t.reshape(B, hw, N_HEADS, d3).transpose(0, 2, 1, 3)
        Q, K, V = jnp.split(t, 3, axis=-1)
        S = jnp.einsum('bhqd,bhkd->bhqk', Q, K) / scale
        A = jax.nn.softmax(S, axis=-1)
        O = jnp.einsum('bhqk,bhkd->bhqd', A, V)
        O = O.transpose(0, 2, 1, 3).reshape(B, hw, C)
        O = O @ Wproj.T + bproj
        return O.transpose(0, 2, 1).reshape(B, C, H, W)

    def _L0_ffn_ref(x, qidx, scales, W):
        import jax, jax.numpy as jnp
        import numpy as np
        BLOCK = 16
        NF4_TABLE = jnp.array([-1.0, -0.6961928009986877, -0.5250730514526367, -0.39491748809814453, -0.28444138169288635, -0.18477343022823334, -0.09105003625154495, 0.0, 0.07958029955625534, 0.16093020141124725, 0.24611230194568634, 0.33791524171829224, 0.44070982933044434, 0.5626170039176941, 0.7229568362236023, 1.0], dtype=jnp.float32)

        def _dequant_nf4(qidx, scales):
            w = NF4_TABLE[qidx].reshape(-1, BLOCK) * scales[:, None]
            return w.reshape(qidx.shape)
        w_lora = _dequant_nf4(qidx, scales)
        y = jnp.einsum('bsd,od->bso', x, w_lora)
        out = jnp.einsum('bsd,od->bso', y, W)
        return out

    def _gn(v, G=32, eps=1e-05):
        B_, C_, H_, W_ = v.shape
        g = v.reshape(B_, G, C_ // G, H_, W_)
        m = jnp.mean(g, axis=(2, 3, 4), keepdims=True)
        s = jnp.var(g, axis=(2, 3, 4), keepdims=True)
        return ((g - m) / jnp.sqrt(s + eps)).reshape(v.shape)

    def _ln_c(v, eps=1e-06):
        m = jnp.mean(v, axis=1, keepdims=True)
        s = jnp.var(v, axis=1, keepdims=True)
        return (v - m) / jnp.sqrt(s + eps)

    def _ln_t(v, eps=1e-05):
        m = jnp.mean(v, axis=-1, keepdims=True)
        s = jnp.var(v, axis=-1, keepdims=True)
        return (v - m) / jnp.sqrt(s + eps)

    def _to_tokens(v):
        B_, C_, H_, W_ = v.shape
        return v.reshape(B_, C_, H_ * W_).transpose(0, 2, 1)

    def _from_tokens(t, like):
        B_, C_, H_, W_ = like.shape
        return t.transpose(0, 2, 1).reshape(B_, C_, H_, W_)
    x = x + _L0_conv_ref(_ln_c(x), L0_conv_gamma, L0_conv_beta, L0_conv_Wqkv, L0_conv_bqkv, L0_conv_Wproj, L0_conv_bproj)
    t = _to_tokens(x)
    t = t + _L0_ffn_ref(_ln_t(t), L0_ffn_qidx, L0_ffn_scales, L0_ffn_W)
    x = _from_tokens(t, x)
    return x

_drawn_inputs = setup_inputs


def setup_inputs(seed=0):
    import zlib

    import numpy as np

    out = dict(_drawn_inputs(seed))
    spreads = {'L0_conv_gamma': (1.0, 0.6),
     'L0_conv_beta': (0.0, 0.8),
     'L0_conv_bqkv': (0.0, 0.304),
     'L0_conv_bproj': (0.0, 0.1)}
    factors = {'L0_conv_Wqkv': 8.0}
    for name, (base, spread) in spreads.items():
        noise = np.random.default_rng([zlib.crc32(name.encode()), seed]).standard_normal(out[name].shape)
        drawn = base * np.exp(spread * noise) if base else spread * noise
        out[name] = jnp.asarray(drawn.astype(out[name].dtype))
    for name, factor in factors.items():
        out[name] = (out[name] * factor).astype(out[name].dtype)
    return out
```

```python
from contextlib import ExitStack

import concourse.bass as bass
from concourse import mybir

ALU = mybir.AluOpType
ACT = mybir.ActivationFunctionType
AX_X = mybir.AxisListType.X
F32 = mybir.dt.float32
F32R = mybir.dt.float32r
I32 = mybir.dt.int32

NF4 = [-1.0, -0.6961928009986877, -0.5250730514526367, -0.39491748809814453, -0.28444138169288635,
       -0.18477343022823334, -0.09105003625154495, 0.0, 0.07958029955625534, 0.16093020141124725,
       0.24611230194568634, 0.33791524171829224, 0.44070982933044434, 0.5626170039176941,
       0.7229568362236023, 1.0]
NF4_BLOCK = 16
EPS_CHANNEL = 1e-6
EPS_ATTN = 1e-5
EPS_FFN = 1e-5


def metaformer_kernel(nc, x, gamma, beta, wqkv, bqkv, wproj, bproj, qidx, scales, wffn, out):
    B, C, HH, WW = x.shape
    T = HH * WW
    NH = 8
    D = C // NH
    P = 128
    NT = T // P
    TERMS = 4
    SROWS = TERMS * D
    MROWS = 2
    GH = 4
    NG = NH // GH
    NGRP = B * NG
    UH = 2
    NU = B * NH // UH
    NB = B * NH
    LAG = 4
    NE = 4
    EW = UH * NT * T
    assert C == P and NT == 2 and D == 16 and T == 256

    x_v = x.rearrange("b c h w -> b c (h w)")
    out_v = out.rearrange("b c h w -> b c (h w)")
    col = lambda v: v.rearrange("(c a) -> c a", a=1)

    with ExitStack() as ctx:
        def sb(name, shape, dt=F32):
            return ctx.enter_context(nc.sbuf_tensor(name, shape, dt))

        def pb(name, shape):
            return ctx.enter_context(nc.psum_tensor(name, shape, F32))

        def sem(name):
            return ctx.enter_context(nc.semaphore(name))

        xs = sb("xs", [P, B, T])
        xb = sb("xb", [P, B, T])
        ident = sb("ident", [P, P])
        gcol, bcol, bpcol = sb("gcol", [P, 1]), sb("bcol", [P, 1]), sb("bpcol", [P, 1])
        bqk = sb("bqk", [P, 2])
        bv = sb("bv", [P, NH, D])
        wqkv_n = sb("wqkv_n", [P, 3, C])
        wproj_n, wffn_n = sb("wproj_n", [P, C]), sb("wffn_n", [P, C])
        wqk_t = sb("wqk_t", [P, 2, D, NH])
        wv_t = sb("wv_t", [P, NH, D])
        wproj_t, wffn_t = sb("wproj_t", [P, C]), sb("wffn_t", [P, C])
        qidx_i, qidx_f = sb("qidx_i", [P, C], I32), sb("qidx_f", [P, C])
        scale_s = sb("scale_s", [P, C // NF4_BLOCK])
        pick = sb("pick", [P, 2, C])
        lora = sb("lora", [P, 2, C])
        lora_s = sb("lora_s", [P, C // NF4_BLOCK, NF4_BLOCK])
        w2_t = sb("w2_t", [P, C])
        eps1, eps2 = sb("eps1", [P, 1]), sb("eps2", [P, 1])
        st6 = sb("st6", [P, 2, B, NT, 6])
        mv = sb("mv", [P, 2, B, NT, 2])
        lnv = sb("lnv", [P, 2, B, NT])
        rstd = sb("rstd", [P, 2, B, NT])
        tn = sb("tn", [P, 2, NT, C])
        tc = sb("tc", [P, 2, T])
        KHI, KLO, QHI, QLO = range(4)
        hl = sb("hl", [P, B, 4, T], F32R)
        K, Q = 0, 1
        stk = sb("stk", [SROWS + MROWS, B, NH, 2, T], F32R)
        vp = sb("vp", [P, B, NT, NH, 32])
        mx = sb("mx", [P, 2, NT, GH])
        nm = sb("nm", [P, 2, NT, MROWS, GH], F32R)
        mt = sb("mt", [MROWS * GH, 2, T], F32R)
        ex = sb("ex", [P, NE, UH, NT, T])
        os_ = sb("os_", [P, 2, NG, T])
        rden = sb("rden", [P, 2, NT, NH])
        on = sb("on", [P, 2, NT, NH, D])
        ot = sb("ot", [P, 2, T])
        t2n = sb("t2n", [P, 2, NT, C])
        t2c = sb("t2c", [P, 2, T])
        res = sb("res", [P, B, T])

        SE = pb("SE", [P, 2, 2 * 512])
        SM = pb("SM", [P, 2, 512])
        OB = pb("OB", [P, NG, T])
        TB = pb("TB", [P, 512])

        def front(b):
            return SE[:, b // 2, (b % 2) * 512:(b % 2 + 1) * 512]

        x_in = [sem(f"x_in{b}") for b in range(B)]
        wqkv_in, affine_in, bqk_in, bv_in = sem("wqkv_in"), sem("affine_in"), sem("bqk_in"), sem("bv_in")
        wproj_in, wffn_in, nf4_in, bproj_in = sem("wproj_in"), sem("wffn_in"), sem("nf4_in"), sem("bproj_in")
        ident_zero, ident_ok, eps_ok = sem("ident_zero"), sem("ident_ok"), sem("eps_ok")
        ones_ok, vones_ok, xb_ok = sem("ones_ok"), sem("vones_ok"), sem("xb_ok")
        nf4_step, lora_ok = sem("nf4_step"), sem("lora_ok")
        pe_w, w_ok, pe_w2, w2_ok, pe_wx, wx_ok = (sem(n) for n in ("pe_w", "w_ok", "pe_w2", "w2_ok", "pe_wx", "wx_ok"))
        pe_xt, bn1, mv1, ln1, r1, tn_ok = (sem(n) for n in ("pe_xt", "bn1", "mv1", "ln1", "r1", "tn_ok"))
        pe_tc, tc_ok, pe_qk, hi_ok, lo_ok = (sem(n) for n in ("pe_tc", "tc_ok", "pe_qk", "hi_ok", "lo_ok"))
        pe_v, v_ok = sem("pe_v"), sem("v_ok")
        stk_sp = [sem(f"stk_sp{b}") for b in range(B)]
        stk_pool = [sem(f"stk_pool{b}") for b in range(B)]
        pe_max, max_ok, nmh_ok, nml_ok = sem("pe_max"), sem("max_ok"), sem("nmh_ok"), sem("nml_ok")
        pe_mt, mt_ok = sem("pe_mt"), sem("mt_ok")
        m_in = [sem("m_in0"), sem("m_in1")]
        pe_s, ex_ok, pe_av, os_ok = sem("pe_s"), sem("ex_ok"), sem("pe_av"), sem("os_ok")
        pe_on, rden_ok, on_ok, pe_ot, ot_ok = (sem(n) for n in ("pe_on", "rden_ok", "on_ok", "pe_ot", "ot_ok"))
        pe_x1, bn2, mv2, ln2, r2, t2n_ok = (sem(n) for n in ("pe_x1", "bn2", "mv2", "ln2", "r2", "t2n_ok"))
        pe_t2, t2c_ok, pe_f, res_ok = (sem(n) for n in ("pe_t2", "t2c_ok", "pe_f", "res_ok"))
        stored = sem("stored")

        def exp_unit(s):
            return s - LAG if 0 <= s - LAG < NU else None

        def av_group(s):
            g, odd = divmod(s - LAG - 2, 2)
            return g if not odd and 0 <= g < NGRP else None

        def mt_group(s):
            g, odd = divmod(s - 2, 2)
            return g if not odd and 0 <= g < NGRP else None

        def tail(s, k):
            b, r = divmod(s - k - (LAG + 4), 2 * NG)
            return b if r == 0 and 0 <= b < B else None

        STEPS = NU + LAG + 8
        W2_STEP = LAG + 3

        block = ctx.enter_context(nc.Block())

        @block.sync
        def _(sp):
            def store(b):
                sp.wait_ge(res_ok, b + 1)
                sp.dma_start(out_v[b], res[:, b, :]).then_inc(stored, 16)

            sp.dma_start(xs[:, 0, :], x_v[0]).then_inc(x_in[0], 16)
            sp.dma_start(wqkv_n[:, :, :], wqkv.rearrange("(a p) c -> p a c", p=P)).then_inc(wqkv_in, 16)
            for b in range(1, B):
                sp.dma_start(xs[:, b, :], x_v[b]).then_inc(x_in[b], 16)
            for b in range(B):
                sp.wait_ge(hi_ok, 2 * b + 2)
                sp.dma_start(stk[0:D, b, :, :, :].bitcast(F32), hl[:, b, KHI:QHI + 1:2, :].bitcast(F32)).then_inc(stk_sp[b], 16)
                sp.wait_ge(lo_ok, 2 * b + 2)
                sp.dma_start(stk[D:2 * D, b, :, :, :].bitcast(F32), hl[:, b, KLO:QHI + 1, :].bitcast(F32)).then_inc(stk_sp[b], 16)
            for g in range(NGRP):
                b, h0 = g // NG, GH * (g % NG)
                sp.wait_ge(mt_ok, g + 1)
                sp.dma_start(stk[SROWS:SROWS + MROWS, b, h0:h0 + GH, Q, :].bitcast(F32), mt[:, g % 2, :].bitcast(F32)).then_inc(m_in[g % 2], 16)
                if g == NGRP - 2:
                    store(0)
            for b in range(1, B):
                store(b)
            sp.wait_ge(stored, 16 * B)

        @block.gpsimd
        def _(pool):
            with nc.allow_non_contiguous_dma(reason="small vector, one element per partition"):
                for part in (0, 1):
                    pool.dma_start(bqk[:, part:part + 1], bqkv.rearrange("(h p d a) -> p d h a", h=NH, p=3, a=1)[part]).then_inc(bqk_in, 16)
                pool.dma_start(bpcol[:, :], col(bproj)).then_inc(bproj_in, 16)
            pool.memset(ident[:, :], 0.0).then_inc(ident_zero, 1)
            pool.wait_ge(ident_zero, 1)
            pool.affine_select(out=ident[:, :], in_=ident[:, :], compare_op=ALU.not_equal, fill=1.0, base=0,
                               pattern=[[-1, P]], channel_multiplier=1).then_inc(ident_ok, 1)
            pool.dma_start(qidx_i[:, :], qidx).then_inc(nf4_in, 16)
            pool.dma_start(scale_s[:, :], scales.rearrange("(o j) -> o j", o=P)).then_inc(nf4_in, 16)
            pool.memset(vp[:, :, :, :, D:32].rearrange("p b t h d -> p (b t h) d"), 1.0).then_inc(vones_ok, 1)
            for b in range(B):
                pool.wait_ge(hi_ok, 2 * b + 2)
                pool.wait_ge(lo_ok, 2 * b + 2)
                pool.dma_start(stk[2 * D:3 * D, b, :, :, :].bitcast(F32), hl[:, b, KHI:QLO + 1:3, :].bitcast(F32)).then_inc(stk_pool[b], 16)
                pool.dma_start(stk[3 * D:4 * D, b, :, :, :].bitcast(F32), hl[:, b, KLO:QLO + 1:2, :].bitcast(F32)).then_inc(stk_pool[b], 16)
                if b == 0:
                    pool.wait_ge(vones_ok, 1)
                    for c in range(B):
                        if c:
                            pool.wait_ge(ones_ok, c)
                        pool.memset(stk[SROWS:SROWS + MROWS, c, :, K, :].bitcast(F32), 1.0).then_inc(ones_ok, 1)
            pool.wait_ge(ones_ok, B)
            pool.wait_ge(nf4_in, 32)
            pool.tensor_copy(qidx_f[:, :], qidx_i[:, :]).then_inc(nf4_step, 1)
            pool.wait_ge(nf4_step, 1)
            n = 1
            for k, value in enumerate(NF4):
                dst = lora[:, 0, :] if k == 0 else pick[:, k % 2, :]
                pool.tensor_scalar(dst, qidx_f[:, :], float(k), value, ALU.is_equal, ALU.mult).then_inc(nf4_step, 1)
                n += 1
                pool.wait_ge(nf4_step, n)
                if k:
                    pool.tensor_tensor(lora[:, k % 2, :], lora[:, (k - 1) % 2, :], dst, ALU.add).then_inc(nf4_step, 1)
                    n += 1
                    pool.wait_ge(nf4_step, n)
            last = lora[:, (len(NF4) - 1) % 2, :].rearrange("o (j k) -> o j k", k=NF4_BLOCK)
            pool.tensor_tensor(lora_s[:, :, :], last,
                               scale_s[:, :].unsqueeze(2).to_broadcast([P, C // NF4_BLOCK, NF4_BLOCK]),
                               ALU.mult).then_inc(lora_ok, 1)
            pool.wait_ge(bproj_in, 16)
            for b in range(B):
                pool.wait_ge(x_in[b], 16)
                pool.tensor_scalar(xb[:, b, :], xs[:, b, :], bpcol[:, 0:1], None, ALU.add).then_inc(xb_ok, 1)

        @block.scalar
        def _(act):
            with nc.allow_non_contiguous_dma(reason="small vectors, one element per partition"):
                act.dma_start(gcol[:, :], col(gamma)).then_inc(affine_in, 16)
                act.dma_start(bcol[:, :], col(beta)).then_inc(affine_in, 16)
            act.preload_act_table_set("natural_log_exp_and_others")
            act.dma_start(bv[:, :, :], bqkv.rearrange("(h p d) -> p h d", h=NH, p=3)[2].partition_broadcast(P)).then_inc(bv_in, 16)
            act.dma_start(wproj_n[:, :], wproj).then_inc(wproj_in, 16)
            act.dma_start(wffn_n[:, :], wffn).then_inc(wffn_in, 16)
            act.wait_ge(eps_ok, 2)

            def norm1_rstd(b):
                act.wait_ge(mv1, NT * (b + 1))
                act.activation(lnv[:, 0, b, :], mv[:, 0, b, :, 1], ACT.Ln, bias=eps1[:, 0:1], scale=1.0 + EPS_ATTN).then_inc(ln1, 1)
                act.wait_ge(ln1, b + 1)
                act.activation(rstd[:, 0, b, :], lnv[:, 0, b, :], ACT.Exp, scale=-0.5).then_inc(r1, 1)

            def affine(b):
                act.wait_ge(pe_tc, b + 1)
                if b == 0:
                    act.wait_ge(affine_in, 32)
                if b >= 2:
                    act.wait_ge(pe_v, b - 1)
                act.activation(tc[:, b % 2, :], front(b)[:, T:2 * T], ACT.Identity, bias=bcol[:, 0:1],
                               scale=gcol[:, 0:1]).then_inc(tc_ok, 1)

            def split_hi(b):
                act.wait_ge(pe_qk, b + 1)
                if b == 0:
                    act.wait_ge(bqk_in, 32)
                act.activation(hl[:, b, KHI, :], SM[:, b % 2, 0:T], ACT.Identity, bias=bqk[:, 1:2]).then_inc(hi_ok, 1)
                act.activation(hl[:, b, QHI, :], SM[:, b % 2, T:2 * T], ACT.Identity, bias=bqk[:, 0:1]).then_inc(hi_ok, 1)

            norm1_rstd(0)
            norm1_rstd(1)
            affine(0)
            split_hi(0)
            norm1_rstd(2)
            affine(1)
            split_hi(1)
            norm1_rstd(3)
            affine(2)
            split_hi(2)
            affine(3)
            split_hi(3)
            act.wait_ge(pe_wx, 1)
            act.activation(wproj_t[:, :], OB[:, 0, 0:C], ACT.Copy).then_inc(wx_ok, 1)
            act.activation(wffn_t[:, :], OB[:, 0, C:2 * C], ACT.Copy).then_inc(wx_ok, 1)

            for s in range(STEPS):
                u = exp_unit(s)
                if u is not None:
                    act.wait_ge(pe_s, u + 1)
                    if u >= NE:
                        act.wait_ge(pe_av, (u - NE) // 2 + 1)
                    act.activation(ex[:, u % NE, :, :, :].rearrange("p h t q -> p (h t q)"), SE[:, u % 2, :], ACT.Exp,
                                   scale=float(D) ** -0.5).then_inc(ex_ok, 1)
                b = tail(s, 0)
                if b is not None:
                    act.wait_ge(pe_av, NG * (b + 1))
                    if b >= 2:
                        act.wait_ge(pe_on, b - 1)
                    act.activation(os_[:, b % 2, :, :], OB[:, :, :], ACT.Copy).then_inc(os_ok, 1)
                b = tail(s, 2)
                if b is not None:
                    act.wait_ge(pe_ot, b + 1)
                    if b >= 2:
                        act.wait_ge(pe_f, b - 1)
                    act.activation(ot[:, b % 2, :], TB[:, 0:T], ACT.Copy).then_inc(ot_ok, 1)
                b = tail(s, 3)
                if b is not None:
                    act.wait_ge(mv2, NT * (b + 1))
                    act.activation(lnv[:, 1, b, :], mv[:, 1, b, :, 1], ACT.Ln, bias=eps2[:, 0:1]).then_inc(ln2, 1)
                    act.wait_ge(ln2, b + 1)
                    act.activation(rstd[:, 1, b, :], lnv[:, 1, b, :], ACT.Exp, scale=-0.5).then_inc(r2, 1)
                b = tail(s, 4)
                if b is not None:
                    act.wait_ge(pe_t2, b + 1)
                    if b >= 2:
                        act.wait_ge(pe_f, b - 1)
                    act.activation(t2c[:, b % 2, :], TB[:, 0:T], ACT.Copy).then_inc(t2c_ok, 1)

        @block.vector
        def _(dve):
            dve.memset(eps1[:, :], EPS_ATTN * EPS_CHANNEL).then_inc(eps_ok, 1)
            dve.memset(eps2[:, :], EPS_FFN).then_inc(eps_ok, 1)

            def stats(which, b, src, bn, mvs):
                for t in range(NT):
                    dve.bn_stats(st6[:, which, b, t, :], src[:, t * C:(t + 1) * C]).then_inc(bn, 1)
                for t in range(NT):
                    dve.wait_ge(bn, NT * b + t + 1)
                    dve.bn_aggr(mv[:, which, b, t, :], st6[:, which, b, t, :]).then_inc(mvs, 1)

            def normalize(which, b, dst, src, r, done):
                dve.wait_ge(r, b + 1)
                for t in range(NT):
                    dve.tensor_scalar(dst[:, b % 2, t, :], src[:, t * C:(t + 1) * C], mv[:, which, b, t, 0:1],
                                      rstd[:, which, b, t:t + 1], ALU.subtract, ALU.mult).then_inc(done, 1)

            def norm1_stats(b):
                dve.wait_ge(pe_xt, b + 1)
                stats(0, b, front(b), bn1, mv1)

            def norm1_apply(b):
                if b >= 2:
                    dve.wait_ge(pe_tc, b - 1)
                normalize(0, b, tn, front(b), r1, tn_ok)

            def split_lo(b):
                dve.wait_ge(hi_ok, 2 * b + 2)
                for i, (hi, lo) in enumerate(((KHI, KLO), (QHI, QLO))):
                    dve.scalar_tensor_tensor(out=hl[:, b, lo, :], in0=SM[:, b % 2, i * T:(i + 1) * T],
                                             scalar=bqk[:, 1 - i:2 - i], in1=hl[:, b, hi, :].bitcast(F32),
                                             op0=ALU.add, op1=ALU.subtract).then_inc(lo_ok, 1)

            def v_bias(b):
                dve.wait_ge(pe_v, b + 1)
                if b == 0:
                    dve.wait_ge(bv_in, 16)
                for t in range(NT):
                    dve.tensor_tensor(vp[:, b, t, :, 0:D],
                                      front(b)[:, t * C:(t + 1) * C].rearrange("p (h d) -> p h d", h=NH),
                                      bv[:, :, :], ALU.add).then_inc(v_ok, 1)

            def evac_mt(g):
                dve.wait_ge(pe_mt, g + 1)
                if g >= 2:
                    dve.wait_ge(m_in[g % 2], 16 * (g // 2))
                dve.tensor_copy(mt[:, g % 2, :], TB[0:MROWS * GH, 0:T]).then_inc(mt_ok, 1)

            norm1_stats(0)
            dve.wait_ge(pe_w, 1)
            wt = TB[:, 0:3 * C].rearrange("c (h p d) -> c p d h", h=NH, p=3)
            dve.tensor_copy(wqk_t[:, :, :, :], wt[:, 0:2]).then_inc(w_ok, 1)
            dve.tensor_copy(wv_t[:, :, :], TB[:, 0:3 * C].rearrange("c (h p d) -> c p h d", h=NH, p=3)[:, 2]).then_inc(w_ok, 1)
            norm1_apply(0)
            norm1_stats(1)
            norm1_apply(1)
            split_lo(0)
            norm1_stats(2)
            norm1_apply(2)
            v_bias(0)
            split_lo(1)
            norm1_stats(3)
            norm1_apply(3)
            v_bias(1)
            split_lo(2)
            v_bias(2)
            split_lo(3)
            v_bias(3)

            for s in range(STEPS):
                for v in (2 * s, 2 * s + 1):
                    if v >= NB:
                        break
                    g = v // GH
                    dve.wait_ge(pe_max, v + 1)
                    if g >= 2 and v % GH == 0:
                        dve.wait_ge(nml_ok, g - 1)
                    dve.tensor_reduce(mx[:, g % 2, :, v % GH], SM[:, v % 2, :].rearrange("p (t k) -> p t k", t=NT),
                                      AX_X, ALU.max).then_inc(max_ok, 1)
                    if v % GH == GH - 1:
                        dve.wait_ge(max_ok, v + 1)
                        if g >= 2:
                            dve.wait_ge(pe_mt, g - 1)
                        m = mx[:, g % 2, :, :]
                        hi, lo = nm[:, g % 2, :, 0, :], nm[:, g % 2, :, 1, :]
                        dve.tensor_scalar(hi, m, -1.0, None, ALU.mult).then_inc(nmh_ok, 1)
                        dve.wait_ge(nmh_ok, g + 1)
                        dve.scalar_tensor_tensor(out=lo, in0=m, scalar=-1.0, in1=hi.bitcast(F32),
                                                 op0=ALU.mult, op1=ALU.subtract).then_inc(nml_ok, 1)
                    if v % 2 == 0 and mt_group(s) is not None:
                        evac_mt(mt_group(s))
                if 2 * s >= NB and mt_group(s) is not None:
                    evac_mt(mt_group(s))
                if s == W2_STEP:
                    dve.wait_ge(pe_w2, 1)
                    dve.tensor_copy(w2_t[:, :], TB[:, 0:C]).then_inc(w2_ok, 1)
                b = tail(s, 5)
                if b is not None:
                    dve.wait_ge(pe_f, b + 1)
                    dve.wait_ge(xb_ok, b + 1)
                    dve.tensor_tensor(res[:, b, :], TB[:, 0:T], xb[:, b, :], ALU.add).then_inc(res_ok, 1)
                b = tail(s, 1)
                if b is not None:
                    o = TB[:, :].rearrange("p (t h e) -> p t h e", t=NT, h=NH)
                    dve.wait_ge(pe_on, b + 1)
                    dve.reciprocal(rden[:, b % 2, :, :], o[:, :, :, D]).then_inc(rden_ok, 1)
                    dve.wait_ge(rden_ok, b + 1)
                    for t in range(NT):
                        dve.tensor_tensor(on[:, b % 2, t, :, :], o[:, t, :, 0:D],
                                          rden[:, b % 2, t, :].unsqueeze(2).to_broadcast([P, NH, D]),
                                          ALU.mult).then_inc(on_ok, 1)
                b = tail(s, 3)
                if b is not None:
                    dve.wait_ge(pe_x1, b + 1)
                    stats(1, b, TB, bn2, mv2)
                    normalize(1, b, t2n, TB, r2, t2n_ok)

        @block.tensor
        def _(pe):
            free_tb = []

            def take_tb(sem_, value):
                if free_tb:
                    pe.wait_ge(*free_tb.pop())
                free_tb.append((sem_, value))

            def turn(dst, src):
                return pe.transpose(dst, src, ident[:, :])

            def x_turn(b):
                pe.wait_ge(x_in[b], 16)
                for t in range(NT):
                    last = turn(front(b)[:, t * C:(t + 1) * C], xs[:, b, t * P:(t + 1) * P])
                last.then_inc(pe_xt, 1)

            def t_turn(b):
                pe.wait_ge(tn_ok, NT * (b + 1))
                for t in range(NT):
                    last = turn(front(b)[:, T + t * P:T + (t + 1) * P], tn[:, b % 2, t, :])
                last.then_inc(pe_tc, 1)

            def project(b):
                pe.wait_ge(tc_ok, b + 1)
                if b == 0:
                    pe.wait_ge(w_ok, 2)
                if b >= 2:
                    pe.wait_ge(lo_ok, 2 * (b - 1))
                for i, part in enumerate((1, 0)):
                    last = pe.matmul(SM[:, b % 2, i * T:(i + 1) * T],
                                     wqk_t[:, part, :, :].rearrange("c d h -> c (d h)"), tc[:, b % 2, :],
                                     start=True, stop=True)
                last.then_inc(pe_qk, 1)
                for t in range(NT):
                    last = pe.matmul(front(b)[:, t * C:(t + 1) * C], tc[:, b % 2, t * P:(t + 1) * P],
                                     wv_t[:, :, :].rearrange("c h d -> c (h d)"), start=True, stop=True)
                last.then_inc(pe_v, 1)

            pe.wait_ge(ident_ok, 1)
            x_turn(0)
            pe.wait_ge(wqkv_in, 16)
            take_tb(w_ok, 2)
            for a in range(3):
                last = turn(TB[:, a * C:(a + 1) * C], wqkv_n[:, a, :])
            last.then_inc(pe_w, 1)
            x_turn(1)
            t_turn(0)
            x_turn(2)
            x_turn(3)
            project(0)
            t_turn(1)
            project(1)
            t_turn(2)
            project(2)
            t_turn(3)
            project(3)
            pe.wait_ge(wproj_in, 16)
            pe.wait_ge(wffn_in, 16)
            turn(OB[:, 0, 0:C], wproj_n[:, :])
            turn(OB[:, 0, C:2 * C], wffn_n[:, :]).then_inc(pe_wx, 1)

            def max_scores(v):
                b, h = divmod(v, NH)
                if v < 2:
                    pe.wait_ge(lo_ok, 2 * B)
                else:
                    pe.wait_ge(max_ok, v - 1)
                if h == 0:
                    pe.wait_ge(stk_sp[b], 32)
                    pe.wait_ge(stk_pool[b], 32)
                for t in range(NT):
                    last = pe.matmul(SM[:, v % 2, t * T:(t + 1) * T], stk[0:SROWS, b, h, Q, t * P:(t + 1) * P],
                                     stk[0:SROWS, b, h, K, :], start=True, stop=True)
                last.then_inc(pe_max, 1)

            def exp_scores(u):
                b, h0 = divmod(UH * u, NH)
                if u < 2:
                    pe.wait_ge(v_ok, 2 * NT * (u + 1))
                else:
                    pe.wait_ge(ex_ok, u - 1)
                if u == 0:
                    pe.wait_ge(ones_ok, B)
                g = UH * u // GH
                pe.wait_ge(m_in[g % 2], 16 * (g // 2 + 1))
                for i in range(UH):
                    for t in range(NT):
                        last = pe.matmul(SE[:, u % 2, (i * NT + t) * T:(i * NT + t + 1) * T],
                                         stk[:, b, h0 + i, K, t * P:(t + 1) * P], stk[:, b, h0 + i, Q, :],
                                         start=True, stop=True)
                last.then_inc(pe_s, 1)

            def values(g):
                b, gi = divmod(g, NG)
                pe.wait_ge(ex_ok, 2 * g + 2)
                if g == 0:
                    pe.wait_ge(vones_ok, 1)
                    pe.wait_ge(v_ok, NT * B)
                    pe.wait_ge(wx_ok, 2)
                if gi == 0 and b:
                    pe.wait_ge(os_ok, b)
                for t in range(NT):
                    for i in range(GH):
                        u = 2 * g + i // UH
                        last = pe.matmul(OB[32 * i:32 * i + 32, gi, :], vp[:, b, t, GH * gi + i, :],
                                         ex[:, u % NE, i % UH, t, :], start=(t == 0), stop=(t == NT - 1))
                last.then_inc(pe_av, 1)

            for s in range(STEPS):
                if 2 * s < NB:
                    max_scores(2 * s)
                g = mt_group(s)
                if g is not None:
                    pe.wait_ge(nml_ok, g + 1)
                    take_tb(mt_ok, g + 1)
                    for t in range(NT):
                        last = turn(TB[0:MROWS * GH, t * P:(t + 1) * P],
                                    nm[:, g % 2, t, :, :].rearrange("p s h -> p (s h)").bitcast(F32))
                    last.then_inc(pe_mt, 1)
                if 2 * s < NB:
                    max_scores(2 * s + 1)
                if exp_unit(s) is not None:
                    exp_scores(exp_unit(s))
                if av_group(s) is not None:
                    values(av_group(s))
                if s == W2_STEP:
                    pe.wait_ge(lora_ok, 1)
                    take_tb(w2_ok, 1)
                    pe.matmul(TB[:, 0:C], lora_s[:, :, :].rearrange("o j k -> o (j k)"), wffn_t[:, :],
                              start=True, stop=True).then_inc(pe_w2, 1)
                b = tail(s, 5)
                if b is not None:
                    pe.wait_ge(t2c_ok, b + 1)
                    if b == 0:
                        pe.wait_ge(w2_ok, 1)
                    take_tb(res_ok, b + 1)
                    pe.matmul(TB[:, 0:T], w2_t[:, :], t2c[:, b % 2, :], start=True, stop=False)
                    pe.matmul(TB[:, 0:T], wproj_t[:, :], ot[:, b % 2, :], start=False, stop=True).then_inc(pe_f, 1)
                b = tail(s, 1)
                if b is not None:
                    pe.wait_ge(os_ok, b + 1)
                    take_tb(on_ok, NT * (b + 1))
                    for t in range(NT):
                        for gi in range(NG):
                            last = turn(TB[:, (t * NG + gi) * P:(t * NG + gi + 1) * P],
                                        os_[:, b % 2, gi, t * P:(t + 1) * P])
                    last.then_inc(pe_on, 1)
                b = tail(s, 2)
                if b is not None:
                    pe.wait_ge(on_ok, NT * (b + 1))
                    take_tb(ot_ok, b + 1)
                    for t in range(NT):
                        last = turn(TB[:, t * P:(t + 1) * P], on[:, b % 2, t, :, :].rearrange("p h d -> p (h d)"))
                    last.then_inc(pe_ot, 1)
                b = tail(s, 3)
                if b is not None:
                    pe.wait_ge(ot_ok, b + 1)
                    pe.wait_ge(xb_ok, b + 1)
                    take_tb(t2n_ok, NT * (b + 1))
                    for t in range(NT):
                        pe.matmul(TB[:, t * C:(t + 1) * C], ot[:, b % 2, t * P:(t + 1) * P], wproj_t[:, :],
                                  start=True, stop=False)
                        last = pe.matmul(TB[:, t * C:(t + 1) * C], xb[:, b, t * P:(t + 1) * P], ident[:, :],
                                         start=False, stop=True)
                    last.then_inc(pe_x1, 1)
                b = tail(s, 4)
                if b is not None:
                    pe.wait_ge(t2n_ok, NT * (b + 1))
                    take_tb(t2c_ok, b + 1)
                    for t in range(NT):
                        last = turn(TB[:, t * P:(t + 1) * P], t2n[:, b % 2, t, :])
                    last.then_inc(pe_t2, 1)


_INS = ['x', 'L0_conv_gamma', 'L0_conv_beta', 'L0_conv_Wqkv', 'L0_conv_bqkv', 'L0_conv_Wproj', 'L0_conv_bproj',
        'L0_ffn_qidx', 'L0_ffn_scales', 'L0_ffn_W']


def kernel(**inputs):
    import numpy as _np
    import concourse.bacc as _bacc
    from concourse import mybir as _mybir
    from concourse.bass_utils import run_bass_kernel_spmd as _run

    nc = _bacc.Bacc("TRN2", target_bir_lowering=False, num_devices=1)
    arrays, args = {}, []
    for name in _INS:
        a = _np.ascontiguousarray(inputs[name])
        arrays[f"in_{name}_dram"] = a
        args.append(nc.dram_tensor(f"in_{name}_dram", a.shape, _mybir.dt.from_np(a.dtype), kind="ExternalInput").ap())
    shape = inputs['x'].shape
    out = nc.dram_tensor("out_0_dram", shape, _mybir.dt.float32, kind="ExternalOutput").ap()
    metaformer_kernel(nc, *args, out)
    r = _run(nc, [arrays], core_ids=[0])
    return r.results[0]["out_0_dram"]
```

```python
from contextlib import ExitStack

import concourse.bass as bass
from concourse import mybir

ALU = mybir.AluOpType
ACT = mybir.ActivationFunctionType
AX_X = mybir.AxisListType.X
F32 = mybir.dt.float32
F32R = mybir.dt.float32r
I32 = mybir.dt.int32

NF4 = [-1.0, -0.6961928009986877, -0.5250730514526367, -0.39491748809814453, -0.28444138169288635,
       -0.18477343022823334, -0.09105003625154495, 0.0, 0.07958029955625534, 0.16093020141124725,
       0.24611230194568634, 0.33791524171829224, 0.44070982933044434, 0.5626170039176941,
       0.7229568362236023, 1.0]
NF4_BLOCK = 16
EPS_CHANNEL = 1e-6
EPS_ATTN = 1e-5
EPS_FFN = 1e-5


def metaformer_kernel(nc, x, gamma, beta, wqkv, bqkv, wproj, bproj, qidx, scales, wffn, out):
    B, C, HH, WW = x.shape
    T = HH * WW
    NH = 8
    D = C // NH
    P = 128
    NT = T // P
    TERMS = 4
    SROWS = TERMS * D
    MROWS = 2
    GH = 4
    NG = NH // GH
    NGRP = B * NG
    NB = B * NH
    NM, NX = 3, 2
    EARLY = 2
    LAG = 12
    DVE_FROM = 2
    MT_AT = 8
    NM_STEP = 1
    NE = 8
    assert C == P and NT == 2 and D == 16 and T == 256

    x_v = x.rearrange("b c h w -> b c (h w)")
    out_v = out.rearrange("b c h w -> b c (h w)")
    col = lambda v: v.rearrange("(c a) -> c a", a=1)

    with ExitStack() as ctx:
        def sb(name, shape, dt=F32):
            return ctx.enter_context(nc.sbuf_tensor(name, shape, dt))

        def pb(name, shape):
            return ctx.enter_context(nc.psum_tensor(name, shape, F32))

        def sem(name):
            return ctx.enter_context(nc.semaphore(name))

        xs = sb("xs", [P, B, T])
        xb = sb("xb", [P, B, T])
        ident = sb("ident", [P, P])
        gcol, bcol, bpcol = sb("gcol", [P, 1]), sb("bcol", [P, 1]), sb("bpcol", [P, 1])
        bvcol = sb("bvcol", [P, 1])
        bpv = sb("bpv", [P, 1])
        bqk = sb("bqk", [P, 2])
        wqkv_n = sb("wqkv_n", [P, 3, C])
        wproj_n, wffn_n = sb("wproj_n", [P, C]), sb("wffn_n", [P, C])
        wqk_t = sb("wqk_t", [P, 2, D, NH])
        wv_t = sb("wv_t", [P, NH, D])
        wx_t = sb("wx_t", [P, 2, C])
        wproj_t, wffn_t = wx_t[:, 0, :], wx_t[:, 1, :]
        qidx_i, qidx_f = sb("qidx_i", [P, C], I32), sb("qidx_f", [P, C])
        scale_s = sb("scale_s", [P, C // NF4_BLOCK])
        pick = sb("pick", [P, len(NF4), C])
        lora_s = sb("lora_s", [P, C // NF4_BLOCK, NF4_BLOCK])
        w2_t = sb("w2_t", [P, C])
        eps1, eps2 = sb("eps1", [P, 1]), sb("eps2", [P, 1])
        st6 = sb("st6", [P, 2, B, NT, 6])
        mv = sb("mv", [P, 2, B, NT, 2])
        lnv = sb("lnv", [P, 2, B, NT])
        rstd = sb("rstd", [P, 2, B, NT])
        tn = sb("tn", [P, B, NT, C])
        tc = sb("tc", [P, B, T])
        KHI, KLO, QHI, QLO = range(4)
        hl = sb("hl", [P, B, 4, T], F32R)
        K, Q = 0, 1
        stk = sb("stk", [P, B, NH, 2, T], F32R)
        vp = sb("vp", [P, B, NT, NH, 32])
        mx = sb("mx", [P, 2, NT, GH])
        nm = sb("nm", [P, 2, NT, MROWS, GH], F32R)
        mt = sb("mt", [MROWS * GH, 2, T], F32R)
        ex = sb("ex", [P, NE, NT, T])
        os_ = sb("os_", [P, 2, NG, T])
        rden = sb("rden", [P, 2, NT, NH])
        on = sb("on", [P, 2, NT, NH, D])
        ot = sb("ot", [P, 2, T])
        t2n = sb("t2n", [P, 2, NT, C])
        t2c = sb("t2c", [P, 2, T])
        res = sb("res", [P, B, T])

        SE = pb("SE", [P, NX, NT * T])
        SM = pb("SM", [P, NM, NT * T])
        OB = pb("OB", [P, NG, T])
        TA = pb("TA", [P, 512])
        TB = pb("TB", [P, 512])

        def front(b):
            return (SE[:, 0, :], SE[:, 1, :], OB[:, :, :].rearrange("p g q -> p (g q)"), TA[:, :])[b]

        def qk_bank(b):
            return SM[:, b, :] if b < NM else TB[:, :]

        x_in = [sem(f"x_in{b}") for b in range(B)]
        wqkv_in, affine_in, bqk_in, bv_in = sem("wqkv_in"), sem("affine_in"), sem("bqk_in"), sem("bv_in")
        wproj_in, wffn_in, nf4_in, bproj_in = sem("wproj_in"), sem("wffn_in"), sem("nf4_in"), sem("bproj_in")
        ident_zero, ident_ok, eps_ok = sem("ident_zero"), sem("ident_ok"), sem("eps_ok")
        fill_dve, fill_pool, pe_bpv, bpv_ok = sem("fill_dve"), sem("fill_pool"), sem("pe_bpv"), sem("bpv_ok")
        vones_ok, xb_ok = sem("vones_ok"), sem("xb_ok")
        nf4_step, lora_ok = sem("nf4_step"), sem("lora_ok")
        pe_w, w_ok, pe_w2, w2_ok, pe_wx, wx_ok = (sem(n) for n in ("pe_w", "w_ok", "pe_w2", "w2_ok", "pe_wx", "wx_ok"))
        pe_xt, bn1, mv1, ln1, r1, tn_ok = (sem(n) for n in ("pe_xt", "bn1", "mv1", "ln1", "r1", "tn_ok"))
        pe_tc, tc_ok, pe_qk, hi_ok, lo_ok = (sem(n) for n in ("pe_tc", "tc_ok", "pe_qk", "hi_ok", "lo_ok"))
        pe_v, v_ok = sem("pe_v"), sem("v_ok")
        stk_in = [sem(f"stk_in{b}") for b in range(B)]
        pe_max, max_ok, nmh_ok, nml_ok = sem("pe_max"), sem("max_ok"), sem("nmh_ok"), sem("nml_ok")
        pe_mt, mt_ok = sem("pe_mt"), sem("mt_ok")
        m_in = [sem("m_in0"), sem("m_in1")]
        pe_s, ex_ok, pe_av, os_ok = sem("pe_s"), sem("ex_ok"), sem("pe_av"), sem("os_ok")
        pe_on, rden_ok, on_ok, pe_ot, ot_ok = (sem(n) for n in ("pe_on", "rden_ok", "on_ok", "pe_ot", "ot_ok"))
        pe_x1, bn2, mv2, ln2, r2, t2n_ok = (sem(n) for n in ("pe_x1", "bn2", "mv2", "ln2", "r2", "t2n_ok"))
        pe_t2, t2c_ok, pe_f, res_ok = (sem(n) for n in ("pe_t2", "t2c_ok", "pe_f", "res_ok"))
        stored = sem("stored")

        def max_head(s):
            return s if s < NB else None

        def exp_head(s):
            return s - LAG if 0 <= s - LAG < NB else None

        def group(s, first):
            g, r = divmod(s - first, GH)
            return g if r == 0 and 0 <= g < NGRP else None

        def mt_group(s):
            return group(s, MT_AT)

        def nm_group(v, step):
            return group(v, GH + NM_STEP * step)

        def av_group(s):
            return group(s, LAG + GH + 1)

        ON, OT, X1, LN2, T2, FFN = 1, 3, 5, 6, 8, 10

        def tail(s, at):
            b, r = divmod(s - at - (LAG + NH + 1), NH)
            return b if r == 0 and 0 <= b < B else None

        STEPS = NB + LAG + 1 + FFN + 1
        W2_STEP = LAG + NH

        block = ctx.enter_context(nc.Block())

        def keep_output(eng, copy, s):
            g = av_group(s)
            if g is not None and (g // NG >= DVE_FROM) == (eng is nc.vector):
                b, gi = divmod(g, NG)
                eng.wait_ge(pe_av, g + 1)
                if b >= 2 and gi == 0:
                    eng.wait_ge(pe_on, b - 1)
                copy(os_[:, b % 2, gi, :], OB[:, gi, :]).then_inc(os_ok, 1)

        def keep_ot(eng, copy, s):
            b = tail(s, OT)
            if b is not None and (b >= DVE_FROM) == (eng is nc.vector):
                eng.wait_ge(pe_ot, b + 1)
                if b >= 2:
                    eng.wait_ge(pe_f, b - 1)
                copy(ot[:, b % 2, :], TA[:, 0:T]).then_inc(ot_ok, 1)

        def keep_t2(eng, copy, s):
            b = tail(s, T2)
            if b is not None and (b >= DVE_FROM) == (eng is nc.vector):
                eng.wait_ge(pe_t2, b + 1)
                if b >= 2:
                    eng.wait_ge(pe_f, b - 1)
                copy(t2c[:, b % 2, :], TB[:, 0:T]).then_inc(t2c_ok, 1)

        @block.sync
        def _(sp):
            def store(b):
                sp.wait_ge(res_ok, b + 1)
                sp.dma_start(out_v[b], res[:, b, :]).then_inc(stored, 16)

            sp.dma_start(xs[:, 0, :], x_v[0]).then_inc(x_in[0], 16)
            sp.dma_start(wqkv_n[:, :, :], wqkv.rearrange("(a p) c -> p a c", p=P)).then_inc(wqkv_in, 16)
            sp.dma_start(xs[:, 1, :], x_v[1]).then_inc(x_in[1], 16)
            sp.dma_start(xs[:, 2, :], x_v[2]).then_inc(x_in[2], 16)
            sp.dma_start(xs[:, 3, :], x_v[3]).then_inc(x_in[3], 16)
            with nc.allow_non_contiguous_dma(reason="small vectors, one element per partition"):
                for part in (1, 0):
                    sp.dma_start(bqk[:, part:part + 1], bqkv.rearrange("(h p d a) -> p d h a", h=NH, p=3, a=1)[part]).then_inc(bqk_in, 16)
            sp.dma_start(wproj_n[:, :], wproj).then_inc(wproj_in, 16)
            sp.dma_start(wffn_n[:, :], wffn).then_inc(wffn_in, 16)
            sp.dma_start(qidx_i[:, :], qidx).then_inc(nf4_in, 16)
            sp.dma_start(scale_s[:, :], scales.rearrange("(o j) -> o j", o=P)).then_inc(nf4_in, 16)
            for b in range(B):
                sp.wait_ge(hi_ok, 2 * b + 2)
                sp.dma_start(stk[0:D, b, :, :, :].bitcast(F32), hl[:, b, KHI:QHI + 1:2, :].bitcast(F32)).then_inc(stk_in[b], 16)
                sp.wait_ge(lo_ok, 2 * b + 1)
                sp.dma_start(stk[D:2 * D, b, :, :, :].bitcast(F32), hl[:, b, KLO:QHI + 1, :].bitcast(F32)).then_inc(stk_in[b], 16)
                sp.wait_ge(lo_ok, 2 * b + 2)
                sp.dma_start(stk[2 * D:3 * D, b, :, :, :].bitcast(F32), hl[:, b, KHI:QLO + 1:3, :].bitcast(F32)).then_inc(stk_in[b], 16)
                sp.dma_start(stk[3 * D:4 * D, b, :, :, :].bitcast(F32), hl[:, b, KLO:QLO + 1:2, :].bitcast(F32)).then_inc(stk_in[b], 16)
            for g in range(NGRP):
                b, h0 = g // NG, GH * (g % NG)
                sp.wait_ge(mt_ok, g + 1)
                sp.dma_start(stk[SROWS:SROWS + MROWS, b, h0:h0 + GH, Q, :].bitcast(F32), mt[:, g % 2, :].bitcast(F32)).then_inc(m_in[g % 2], 16)
                if g == NGRP - 2:
                    store(0)
            for b in range(1, B):
                store(b)
            sp.wait_ge(stored, 16 * B)

        @block.gpsimd
        def _(pool):
            pool.memset(ident[:, :], 0.0).then_inc(ident_zero, 1)
            pool.wait_ge(ident_zero, 1)
            pool.affine_select(out=ident[:, :], in_=ident[:, :], compare_op=ALU.not_equal, fill=1.0, base=0,
                               pattern=[[-1, P]], channel_multiplier=1).then_inc(ident_ok, 1)

            def fill(b, part, value, n):
                if n:
                    pool.wait_ge(fill_pool, n)
                pool.memset(stk[SROWS:P, b, :, part, :].bitcast(F32), value).then_inc(fill_pool, 1)

            pool.wait_ge(ident_ok, 1)
            fill(0, Q, 0.0, 0)
            pool.wait_ge(fill_pool, 1)
            pool.memset(vp[:, :, :, :, D:32].rearrange("p b t h d -> p (b t h) d"), 1.0).then_inc(vones_ok, 1)
            with nc.allow_non_contiguous_dma(reason="small vectors, one element per partition"):
                pool.dma_start(bvcol[:, :], bqkv.rearrange("(h p d a) -> p h d a", h=NH, p=3, a=1)[2]).then_inc(bv_in, 16)
                pool.dma_start(bpcol[:, :], col(bproj)).then_inc(bproj_in, 16)
            pool.wait_ge(vones_ok, 1)
            for b in (1, 2):
                fill(b, K, 1.0, 2 * b - 1)
                fill(b, Q, 0.0, 2 * b)
            pool.wait_ge(fill_pool, 5)
            pool.wait_ge(nf4_in, 32)
            pool.tensor_copy(qidx_f[:, :], qidx_i[:, :]).then_inc(nf4_step, 1)
            pool.wait_ge(nf4_step, 1)
            for k, value in enumerate(NF4):
                pool.tensor_scalar(pick[:, k, :], qidx_f[:, :], float(k), value, ALU.is_equal, ALU.mult).then_inc(nf4_step, 1)
            n, half = 1 + len(NF4), len(NF4) // 2
            while half:
                pool.wait_ge(nf4_step, n)
                pool.tensor_tensor(pick[:, 0:half, :], pick[:, 0:half, :], pick[:, half:2 * half, :], ALU.add).then_inc(nf4_step, 1)
                n, half = n + 1, half // 2
            pool.wait_ge(nf4_step, n)
            pool.tensor_tensor(lora_s[:, :, :], pick[:, 0, :].rearrange("o (j k) -> o j k", k=NF4_BLOCK),
                               scale_s[:, :].unsqueeze(2).to_broadcast([P, C // NF4_BLOCK, NF4_BLOCK]),
                               ALU.mult).then_inc(lora_ok, 1)
            pool.wait_ge(lora_ok, 1)
            fill(3, K, 1.0, 5)
            fill(3, Q, 0.0, 6)

        @block.scalar
        def _(act):
            act.preload_act_table_set("natural_log_exp_and_others")
            with nc.allow_non_contiguous_dma(reason="small vectors, one element per partition"):
                act.dma_start(gcol[:, :], col(gamma)).then_inc(affine_in, 16)
                act.dma_start(bcol[:, :], col(beta)).then_inc(affine_in, 16)
            act.wait_ge(eps_ok, 2)

            def norm1_rstd(b):
                act.wait_ge(mv1, NT * (b + 1))
                act.activation(lnv[:, 0, b, :], mv[:, 0, b, :, 1], ACT.Ln, bias=eps1[:, 0:1], scale=1.0 + EPS_ATTN).then_inc(ln1, 1)
                act.wait_ge(ln1, b + 1)
                act.activation(rstd[:, 0, b, :], lnv[:, 0, b, :], ACT.Exp, scale=-0.5).then_inc(r1, 1)

            def affine(b):
                act.wait_ge(pe_tc, b + 1)
                if b == 0:
                    act.wait_ge(affine_in, 32)
                act.activation(tc[:, b, :], front(b)[:, T:2 * T], ACT.Identity, bias=bcol[:, 0:1],
                               scale=gcol[:, 0:1]).then_inc(tc_ok, 1)

            def split_hi(b):
                act.wait_ge(pe_qk, b + 1)
                if b == 0:
                    act.wait_ge(bqk_in, 32)
                act.activation(hl[:, b, KHI, :], qk_bank(b)[:, 0:T], ACT.Identity, bias=bqk[:, 1:2]).then_inc(hi_ok, 1)
                act.activation(hl[:, b, QHI, :], qk_bank(b)[:, T:2 * T], ACT.Identity, bias=bqk[:, 0:1]).then_inc(hi_ok, 1)

            def keep_v(b):
                act.wait_ge(pe_v, b + 1)
                if b == 0:
                    act.wait_ge(vones_ok, 1)
                act.activation(vp[:, b, :, :, 0:D].rearrange("p t h d -> p (t h) d"),
                               front(b)[:, 0:NT * C].rearrange("p (x d) -> p x d", d=D), ACT.Copy).then_inc(v_ok, 1)

            norm1_rstd(0)
            norm1_rstd(1)
            affine(0)
            norm1_rstd(2)
            affine(1)
            split_hi(0)
            norm1_rstd(3)
            affine(2)
            split_hi(1)
            act.wait_ge(pe_wx, 1)
            act.activation(wx_t[:, :, :].rearrange("c a o -> c (a o)"), TB[:, 0:2 * C], ACT.Copy).then_inc(wx_ok, 1)
            affine(3)
            keep_v(0)
            split_hi(2)
            act.wait_ge(pe_bpv, 1)
            act.wait_ge(bproj_in, 16)
            act.activation(bpv[:, :], TB[:, 0:1], ACT.Identity, bias=bpcol[:, 0:1]).then_inc(bpv_ok, 1)
            keep_v(1)
            split_hi(3)
            keep_v(2)
            keep_v(3)
            act.wait_ge(bpv_ok, 1)
            for b in range(B):
                act.wait_ge(x_in[b], 16)
                act.activation(xb[:, b, :], xs[:, b, :], ACT.Identity, bias=bpv[:, 0:1]).then_inc(xb_ok, 1)

            copy = lambda dst, src: act.activation(dst, src, ACT.Copy)
            for s in range(STEPS):
                g = mt_group(s)
                if g is not None:
                    act.wait_ge(pe_mt, g + 1)
                    if g >= 2:
                        act.wait_ge(m_in[g % 2], 16 * (g // 2))
                    act.activation(mt[:, g % 2, :], TA[0:MROWS * GH, 0:T], ACT.Copy).then_inc(mt_ok, 1)
                b = tail(s, LN2)
                if b is not None:
                    act.wait_ge(mv2, NT * (b + 1))
                    act.activation(lnv[:, 1, b, :], mv[:, 1, b, :, 1], ACT.Ln, bias=eps2[:, 0:1]).then_inc(ln2, 1)
                    act.wait_ge(ln2, b + 1)
                    act.activation(rstd[:, 1, b, :], lnv[:, 1, b, :], ACT.Exp, scale=-0.5).then_inc(r2, 1)
                v = exp_head(s)
                if v is not None:
                    act.wait_ge(pe_s, v + 1)
                    if v >= NE:
                        act.wait_ge(pe_av, (v - NE) // GH + 1)
                    act.activation(ex[:, v % NE, :, :].rearrange("p t q -> p (t q)"), SE[:, v % NX, :], ACT.Exp,
                                   scale=float(D) ** -0.5).then_inc(ex_ok, 1)
                keep_output(act, copy, s)
                keep_ot(act, copy, s)
                keep_t2(act, copy, s)

        @block.vector
        def _(dve):
            dve.memset(eps1[:, :], EPS_ATTN * EPS_CHANNEL).then_inc(eps_ok, 1)
            dve.memset(eps2[:, :], EPS_FFN).then_inc(eps_ok, 1)

            dve.memset(stk[SROWS:P, 0, :, K, :].bitcast(F32), 1.0).then_inc(fill_dve, 1)

            def stats(which, b, src, bn, mvs):
                for t in range(NT):
                    dve.bn_stats(st6[:, which, b, t, :], src[:, t * C:(t + 1) * C]).then_inc(bn, 1)
                for t in range(NT):
                    dve.wait_ge(bn, NT * b + t + 1)
                    dve.bn_aggr(mv[:, which, b, t, :], st6[:, which, b, t, :]).then_inc(mvs, 1)

            def normalize(which, b, dst, src, r, done):
                dve.wait_ge(r, b + 1)
                for t in range(NT):
                    dve.tensor_scalar(dst[:, t, :], src[:, t * C:(t + 1) * C], mv[:, which, b, t, 0:1],
                                      rstd[:, which, b, t:t + 1], ALU.subtract, ALU.mult).then_inc(done, 1)

            def norm1_stats(b):
                dve.wait_ge(pe_xt, b + 1)
                stats(0, b, front(b), bn1, mv1)

            def norm1_apply(b):
                normalize(0, b, tn[:, b, :, :], front(b), r1, tn_ok)

            def split_lo(b):
                dve.wait_ge(hi_ok, 2 * b + 2)
                for i, (hi, lo) in enumerate(((KHI, KLO), (QHI, QLO))):
                    dve.scalar_tensor_tensor(out=hl[:, b, lo, :], in0=qk_bank(b)[:, i * T:(i + 1) * T],
                                             scalar=bqk[:, 1 - i:2 - i], in1=hl[:, b, hi, :].bitcast(F32),
                                             op0=ALU.add, op1=ALU.subtract).then_inc(lo_ok, 1)

            def maxima(s):
                v = max_head(s)
                if v is not None:
                    g = v // GH
                    dve.wait_ge(pe_max, v + 1)
                    if g >= 2 and v % GH == 0:
                        dve.wait_ge(nml_ok, g - 1)
                    dve.tensor_reduce(mx[:, g % 2, :, v % GH], SM[:, v % NM, :].rearrange("p (t k) -> p t k", t=NT),
                                      AX_X, ALU.max).then_inc(max_ok, 1)
                g = nm_group(s, 0)
                if g is not None:
                    dve.wait_ge(max_ok, GH * (g + 1))
                    if g >= 2:
                        dve.wait_ge(pe_mt, g - 1)
                    dve.tensor_scalar(nm[:, g % 2, :, 0, :], mx[:, g % 2, :, :], -1.0, None, ALU.mult).then_inc(nmh_ok, 1)
                g = nm_group(s, 1)
                if g is not None:
                    dve.wait_ge(nmh_ok, g + 1)
                    dve.scalar_tensor_tensor(out=nm[:, g % 2, :, 1, :], in0=mx[:, g % 2, :, :], scalar=-1.0,
                                             in1=nm[:, g % 2, :, 0, :].bitcast(F32),
                                             op0=ALU.mult, op1=ALU.subtract).then_inc(nml_ok, 1)

            norm1_stats(0)
            dve.wait_ge(pe_w, 1)
            wt = TB[:, 0:3 * C].rearrange("c (h p d) -> c p d h", h=NH, p=3)
            dve.tensor_copy(wqk_t[:, :, :, :], wt[:, 0:2]).then_inc(w_ok, 1)
            norm1_stats(1)
            norm1_apply(0)
            dve.tensor_copy(wv_t[:, :, :], TB[:, 0:3 * C].rearrange("c (h p d) -> c p h d", h=NH, p=3)[:, 2]).then_inc(w_ok, 1)
            norm1_stats(2)
            norm1_apply(1)
            norm1_stats(3)
            norm1_apply(2)
            split_lo(0)
            norm1_apply(3)
            split_lo(1)
            split_lo(2)
            for s in range(EARLY):
                maxima(s)
            split_lo(3)

            for s in range(STEPS):
                if s >= EARLY:
                    maxima(s)
                if s == W2_STEP:
                    dve.wait_ge(pe_w2, 1)
                    dve.tensor_copy(w2_t[:, :], TB[:, 0:C]).then_inc(w2_ok, 1)
                keep_output(dve, dve.tensor_copy, s)
                keep_ot(dve, dve.tensor_copy, s)
                keep_t2(dve, dve.tensor_copy, s)
                b = tail(s, FFN)
                if b is not None:
                    dve.wait_ge(pe_f, b + 1)
                    dve.wait_ge(xb_ok, b + 1)
                    dve.tensor_tensor(res[:, b, :], TB[:, 0:T], xb[:, b, :], ALU.add).then_inc(res_ok, 1)
                b = tail(s, ON)
                if b is not None:
                    o = TA[:, :].rearrange("p (x e) -> p x e", e=32)
                    den = rden[:, b % 2, :, :].rearrange("p t h -> p (t h)")
                    dve.wait_ge(pe_on, b + 1)
                    dve.reciprocal(den, o[:, :, D]).then_inc(rden_ok, 1)
                    dve.wait_ge(rden_ok, b + 1)
                    dve.tensor_tensor(on[:, b % 2, :, :, :].rearrange("p t h d -> p (t h) d"), o[:, :, 0:D],
                                      den.unsqueeze(2).to_broadcast([P, NT * NH, D]), ALU.mult).then_inc(on_ok, 1)
                b = tail(s, X1)
                if b is not None:
                    dve.wait_ge(pe_x1, b + 1)
                    stats(1, b, TB, bn2, mv2)
                b = tail(s, LN2)
                if b is not None:
                    normalize(1, b, t2n[:, b % 2, :, :], TB, r2, t2n_ok)

        @block.tensor
        def _(pe):
            free = {}

            def take(bank, sem_, value):
                if bank.name in free:
                    pe.wait_ge(*free[bank.name])
                free[bank.name] = (sem_, value)

            def turn(dst, src):
                return pe.transpose(dst, src, ident[:, :])

            def x_turn(b):
                pe.wait_ge(x_in[b], 16)
                for t in range(NT):
                    last = turn(front(b)[:, t * C:(t + 1) * C], xs[:, b, t * P:(t + 1) * P])
                last.then_inc(pe_xt, 1)

            def t_turn(b):
                pe.wait_ge(tn_ok, NT * (b + 1))
                for t in range(NT):
                    last = turn(front(b)[:, T + t * P:T + (t + 1) * P], tn[:, b, t, :])
                last.then_inc(pe_tc, 1)

            def project(b):
                pe.wait_ge(tc_ok, b + 1)
                if b == 0:
                    pe.wait_ge(w_ok, 2)
                if b == NM:
                    take(TB, lo_ok, 2 * B)
                for i, part in enumerate((1, 0)):
                    last = pe.matmul(qk_bank(b)[:, i * T:(i + 1) * T],
                                     wqk_t[:, part, :, :].rearrange("c d h -> c (d h)"), tc[:, b, :],
                                     start=True, stop=True)
                last.then_inc(pe_qk, 1)

            def values_of(b):
                if b == B - 1:
                    take(TA, v_ok, B)
                for t in range(NT):
                    last = pe.matmul(front(b)[:, t * C:(t + 1) * C], tc[:, b, t * P:(t + 1) * P],
                                     wv_t[:, :, :].rearrange("c h d -> c (h d)"), start=True, stop=True)
                last.then_inc(pe_v, 1)

            def keep_warm(n, dst):
                for _ in range(n):
                    turn(dst, ident[:, :])

            def max_scores(v):
                b, h = divmod(v, NH)
                if v < NM:
                    pe.wait_ge(lo_ok, 2 * (v + 1))
                else:
                    pe.wait_ge(max_ok, v - NM + 1)
                if h == 0:
                    pe.wait_ge(stk_in[b], 16 * TERMS)
                    pe.wait_ge(fill_dve, 1)
                    pe.wait_ge(fill_pool, 2 * b + 1)
                for t in range(NT):
                    last = pe.matmul(SM[:, v % NM, t * T:(t + 1) * T], stk[:, b, h, Q, t * P:(t + 1) * P],
                                     stk[:, b, h, K, :], start=True, stop=True)
                last.then_inc(pe_max, 1)

            pe.wait_ge(ident_ok, 1)
            keep_warm(9, SM[:, 2, 0:P])
            x_turn(0)
            pe.wait_ge(wqkv_in, 16)
            take(TB, w_ok, 2)
            for a in range(3):
                last = turn(TB[:, a * C:(a + 1) * C], wqkv_n[:, a, :])
            last.then_inc(pe_w, 1)
            x_turn(1)
            keep_warm(3, SM[:, 2, 0:P])
            x_turn(2)
            t_turn(0)
            keep_warm(1, SM[:, 2, 0:P])
            x_turn(3)
            project(0)
            t_turn(1)
            values_of(0)
            project(1)
            t_turn(2)
            pe.wait_ge(wproj_in, 16)
            pe.wait_ge(wffn_in, 16)
            take(TB, wx_ok, 1)
            turn(TB[:, 0:C], wproj_n[:, :])
            turn(TB[:, C:2 * C], wffn_n[:, :]).then_inc(pe_wx, 1)
            project(2)
            values_of(1)
            t_turn(3)
            pe.wait_ge(wx_ok, 1)
            pe.wait_ge(bv_in, 16)
            take(TB, bpv_ok, 1)
            pe.matmul(TB[:, 0:1], wproj_t, bvcol[:, 0:1], start=True, stop=True).then_inc(pe_bpv, 1)
            max_scores(0)
            project(3)
            max_scores(1)
            values_of(2)
            values_of(3)

            def exp_scores(v):
                b, h = divmod(v, NH)
                if v < NX:
                    pe.wait_ge(v_ok, v + 1)
                else:
                    pe.wait_ge(ex_ok, v - NX + 1)
                if v % GH == 0:
                    g = v // GH
                    pe.wait_ge(m_in[g % 2], 16 * (g // 2 + 1))
                for t in range(NT):
                    last = pe.matmul(SE[:, v % NX, t * T:(t + 1) * T], stk[:, b, h, K, t * P:(t + 1) * P],
                                     stk[:, b, h, Q, :], start=True, stop=True)
                last.then_inc(pe_s, 1)

            def values(g):
                b, gi = divmod(g, NG)
                pe.wait_ge(ex_ok, GH * (g + 1))
                if g == 0:
                    pe.wait_ge(v_ok, B)
                if g:
                    pe.wait_ge(os_ok, g)
                for t in range(NT):
                    for i in range(GH):
                        last = pe.matmul(OB[32 * i:32 * i + 32, gi, :], vp[:, b, t, GH * gi + i, :],
                                         ex[:, (GH * g + i) % NE, t, :], start=(t == 0), stop=(t == NT - 1))
                last.then_inc(pe_av, 1)

            for s in range(STEPS):
                g = mt_group(s)
                if g is not None:
                    pe.wait_ge(nml_ok, g + 1)
                    take(TA, mt_ok, g + 1)
                    for t in range(NT):
                        last = turn(TA[0:MROWS * GH, t * P:(t + 1) * P],
                                    nm[:, g % 2, t, :, :].rearrange("p s h -> p (s h)").bitcast(F32))
                    last.then_inc(pe_mt, 1)
                if s >= EARLY and max_head(s) is not None:
                    max_scores(max_head(s))
                if s < LAG:
                    if s == 0:
                        pe.wait_ge(v_ok, NX)
                    keep_warm(1, SE[:, 1, 0:P])
                if exp_head(s) is not None:
                    exp_scores(exp_head(s))
                if av_group(s) is not None:
                    values(av_group(s))
                if s == W2_STEP:
                    pe.wait_ge(lora_ok, 1)
                    take(TB, w2_ok, 1)
                    pe.matmul(TB[:, 0:C], lora_s[:, :, :].rearrange("o j k -> o (j k)"), wffn_t,
                              start=True, stop=True).then_inc(pe_w2, 1)
                b = tail(s, FFN)
                if b is not None:
                    pe.wait_ge(t2c_ok, b + 1)
                    if b == 0:
                        pe.wait_ge(w2_ok, 1)
                    take(TB, res_ok, b + 1)
                    pe.matmul(TB[:, 0:T], w2_t[:, :], t2c[:, b % 2, :], start=True, stop=False)
                    pe.matmul(TB[:, 0:T], wproj_t, ot[:, b % 2, :], start=False, stop=True).then_inc(pe_f, 1)
                b = tail(s, ON)
                if b is not None:
                    pe.wait_ge(os_ok, NG * (b + 1))
                    take(TA, on_ok, b + 1)
                    for t in range(NT):
                        for gi in range(NG):
                            last = turn(TA[:, (t * NG + gi) * P:(t * NG + gi + 1) * P],
                                        os_[:, b % 2, gi, t * P:(t + 1) * P])
                    last.then_inc(pe_on, 1)
                b = tail(s, OT)
                if b is not None:
                    pe.wait_ge(on_ok, b + 1)
                    take(TA, ot_ok, b + 1)
                    for t in range(NT):
                        last = turn(TA[:, t * P:(t + 1) * P], on[:, b % 2, t, :, :].rearrange("p h d -> p (h d)"))
                    last.then_inc(pe_ot, 1)
                b = tail(s, X1)
                if b is not None:
                    pe.wait_ge(ot_ok, b + 1)
                    pe.wait_ge(xb_ok, b + 1)
                    take(TB, t2n_ok, NT * (b + 1))
                    for t in range(NT):
                        pe.matmul(TB[:, t * C:(t + 1) * C], xb[:, b, t * P:(t + 1) * P], ident[:, :],
                                  is_transpose=True, start=True, stop=False)
                        last = pe.matmul(TB[:, t * C:(t + 1) * C], ot[:, b % 2, t * P:(t + 1) * P], wproj_t,
                                         start=False, stop=True)
                    last.then_inc(pe_x1, 1)
                b = tail(s, T2)
                if b is not None:
                    pe.wait_ge(t2n_ok, NT * (b + 1))
                    take(TB, t2c_ok, b + 1)
                    for t in range(NT):
                        last = turn(TB[:, t * P:(t + 1) * P], t2n[:, b % 2, t, :])
                    last.then_inc(pe_t2, 1)


_INS = ['x', 'L0_conv_gamma', 'L0_conv_beta', 'L0_conv_Wqkv', 'L0_conv_bqkv', 'L0_conv_Wproj', 'L0_conv_bproj',
        'L0_ffn_qidx', 'L0_ffn_scales', 'L0_ffn_W']


def kernel(**inputs):
    import numpy as _np
    import concourse.bacc as _bacc
    from concourse import mybir as _mybir
    from concourse.bass_utils import run_bass_kernel_spmd as _run

    nc = _bacc.Bacc("TRN2", target_bir_lowering=False, num_devices=1)
    arrays, args = {}, []
    for name in _INS:
        a = _np.ascontiguousarray(inputs[name])
        arrays[f"in_{name}_dram"] = a
        args.append(nc.dram_tensor(f"in_{name}_dram", a.shape, _mybir.dt.from_np(a.dtype), kind="ExternalInput").ap())
    shape = inputs['x'].shape
    out = nc.dram_tensor("out_0_dram", shape, _mybir.dt.float32, kind="ExternalOutput").ap()
    metaformer_kernel(nc, *args, out)
    r = _run(nc, [arrays], core_ids=[0])
    return r.results[0]["out_0_dram"]
```

```python
from contextlib import ExitStack

import concourse.bass as bass
from concourse import mybir

ALU = mybir.AluOpType
ACT = mybir.ActivationFunctionType
AX_X = mybir.AxisListType.X
F32 = mybir.dt.float32
F32R = mybir.dt.float32r
I32 = mybir.dt.int32

NF4 = [-1.0, -0.6961928009986877, -0.5250730514526367, -0.39491748809814453, -0.28444138169288635,
       -0.18477343022823334, -0.09105003625154495, 0.0, 0.07958029955625534, 0.16093020141124725,
       0.24611230194568634, 0.33791524171829224, 0.44070982933044434, 0.5626170039176941,
       0.7229568362236023, 1.0]
NF4_BLOCK = 16
EPS_CHANNEL = 1e-6
EPS_ATTN = 1e-5
EPS_FFN = 1e-5


def metaformer_kernel(nc, x, gamma, beta, wqkv, bqkv, wproj, bproj, qidx, scales, wffn, out):
    B, C, HH, WW = x.shape
    T = HH * WW
    NH = 8
    D = C // NH
    P = 128
    NT = T // P
    TERMS = 4
    SROWS = TERMS * D
    MROWS = 2
    GH = 4
    NG = NH // GH
    NGRP = B * NG
    NB = B * NH
    NM, NX = 3, 2
    EARLY = 2
    LAG = 11
    TURN_MAX = 7
    DVE_FROM = NB
    BANKS = NX + NM
    NE = 12
    assert C == P and NT == 2 and D == 16 and T == 256

    x_v = x.rearrange("b c h w -> b c (h w)")
    out_v = out.rearrange("b c h w -> b c (h w)")
    col = lambda v: v.rearrange("(c a) -> c a", a=1)

    with ExitStack() as ctx:
        def sb(name, shape, dt=F32):
            return ctx.enter_context(nc.sbuf_tensor(name, shape, dt))

        def pb(name, shape):
            return ctx.enter_context(nc.psum_tensor(name, shape, F32))

        def sem(name):
            return ctx.enter_context(nc.semaphore(name))

        xs = sb("xs", [P, B, T])
        xb = sb("xb", [P, B, T])
        ident = sb("ident", [P, P])
        gcol, bcol, bpcol = sb("gcol", [P, 1]), sb("bcol", [P, 1]), sb("bpcol", [P, 1])
        bvcol = sb("bvcol", [P, 1])
        bpv = sb("bpv", [P, 1])
        bqk = sb("bqk", [P, 2])
        wqkv_n = sb("wqkv_n", [P, 3, C])
        wproj_n, wffn_n = sb("wproj_n", [P, C]), sb("wffn_n", [P, C])
        wqk_t = sb("wqk_t", [P, 2, D, NH])
        wv_t = sb("wv_t", [P, NH, D])
        wx_t = sb("wx_t", [P, 2, C])
        wproj_t, wffn_t = wx_t[:, 0, :], wx_t[:, 1, :]
        qidx_i, qidx_f = sb("qidx_i", [P, C], I32), sb("qidx_f", [P, C])
        scale_s = sb("scale_s", [P, C // NF4_BLOCK])
        pick = sb("pick", [P, len(NF4), C])
        lora_s = sb("lora_s", [P, C // NF4_BLOCK, NF4_BLOCK])
        w2_t = sb("w2_t", [P, C])
        eps1, eps2 = sb("eps1", [P, 1]), sb("eps2", [P, 1])
        const = sb("const", [P, 2])
        st6 = sb("st6", [P, 2, B, NT, 6])
        mv = sb("mv", [P, 2, B, NT, 2])
        lnv = sb("lnv", [P, 2, B, NT])
        rstd = sb("rstd", [P, 2, B, NT])
        tn = sb("tn", [P, B, NT, C])
        tc = sb("tc", [P, B, T])
        KHI, KLO, QHI, QLO = range(4)
        hl = sb("hl", [P, B, 4, T], F32R)
        K, Q = 0, 1
        stk = sb("stk", [P, B, NH, 2, T], F32R)
        vp = sb("vp", [P, B, NT, NH, 32])
        mx = sb("mx", [P, 2, NT, GH])
        nm = sb("nm", [P, 2, NT, MROWS, GH], F32R)
        mt = sb("mt", [MROWS * GH, 2, T], F32R)
        ex = sb("ex", [P, NE, NT, T])
        os_ = sb("os_", [P, 2, NG, T])
        rden = sb("rden", [P, 2, NT, NH])
        on = sb("on", [P, 2, NT, NH, D])
        ot = sb("ot", [P, 2, T])
        t2n = sb("t2n", [P, 2, NT, C])
        t2c = sb("t2c", [P, 2, T])
        res = sb("res", [P, B, T])

        SE = pb("SE", [P, NX, NT * T])
        SM = pb("SM", [P, NM, NT * T])
        OB = pb("OB", [P, NG, T])
        TA = pb("TA", [P, 512])
        TB = pb("TB", [P, 512])

        def front(b):
            return (SE[:, 0, :], SE[:, 1, :], OB[:, :, :].rearrange("p g q -> p (g q)"), TA[:, :])[b]

        def qk_bank(b):
            return SM[:, b, :] if b < NM else TB[:, :]

        LAST_O, LAST_X1 = (TA[:, :], SM[:, 0, :]), (SM[:, 1, :], SM[:, 2, :])
        LAST_T2, LAST_F = (SE[:, 0, :], SE[:, 1, :]), (TB[:, :], OB[:, :, :].rearrange("p g q -> p (g q)"))

        def exp_bank(v):
            first = NB - LAG + 2
            if v < first:
                return SE[:, v % NX, :], (v - NX if v >= NX else None)
            i = (v - first) % BANKS
            before = v - BANKS if v - BANKS >= first else None
            if i < NM:
                return SM[:, i, :], before
            e = i - NM
            if before is None:
                before = max(w for w in range(first) if w % NX == e)
            return SE[:, e, :], before

        x_in = [sem(f"x_in{b}") for b in range(B)]
        wqkv_in, affine_in, bqk_in, bv_in = sem("wqkv_in"), sem("affine_in"), sem("bqk_in"), sem("bv_in")
        wproj_in, wffn_in, nf4_in, bproj_in = sem("wproj_in"), sem("wffn_in"), sem("nf4_in"), sem("bproj_in")
        ident_zero, ident_ok, eps_ok = sem("ident_zero"), sem("ident_ok"), sem("eps_ok")
        fill_act, const_ok = sem("fill_act"), sem("const_ok")
        fill_dve, fill_pool, pe_bpv, bpv_ok = sem("fill_dve"), sem("fill_pool"), sem("pe_bpv"), sem("bpv_ok")
        vones_ok, xb_ok = sem("vones_ok"), sem("xb_ok")
        nf4_step, lora_ok = sem("nf4_step"), sem("lora_ok")
        pe_w, w_ok, pe_w2, w2_ok, pe_wx, wx_ok = (sem(n) for n in ("pe_w", "w_ok", "pe_w2", "w2_ok", "pe_wx", "wx_ok"))
        pe_xt, bn1, mv1, ln1, r1, tn_ok = (sem(n) for n in ("pe_xt", "bn1", "mv1", "ln1", "r1", "tn_ok"))
        pe_tc, tc_ok, pe_qk, hi_ok, lo_ok = (sem(n) for n in ("pe_tc", "tc_ok", "pe_qk", "hi_ok", "lo_ok"))
        pe_v, v_ok = sem("pe_v"), sem("v_ok")
        stk_in = [sem(f"stk_in{b}") for b in range(B)]
        pe_max, max_ok, nmh_ok, nml_ok = sem("pe_max"), sem("max_ok"), sem("nmh_ok"), sem("nml_ok")
        pe_mt, mt_ok = sem("pe_mt"), sem("mt_ok")
        m_in = [sem("m_in0"), sem("m_in1")]
        pe_s, ex_ok, pe_av, os_ok = sem("pe_s"), sem("ex_ok"), sem("pe_av"), sem("os_ok")
        pe_on, rden_ok, on_ok, pe_ot, ot_ok = (sem(n) for n in ("pe_on", "rden_ok", "on_ok", "pe_ot", "ot_ok"))
        pe_x1, bn2, mv2, ln2, r2, t2n_ok = (sem(n) for n in ("pe_x1", "bn2", "mv2", "ln2", "r2", "t2n_ok"))
        pe_t2, t2c_ok, pe_f, res_ok = (sem(n) for n in ("pe_t2", "t2c_ok", "pe_f", "res_ok"))
        stored = sem("stored")
        (last_on, last_rden, last_norm, last_ot, last_otc, last_x1, last_bn, last_mv, last_ln, last_r, last_t2n,
         last_t2, last_t2c, last_f, last_res) = (sem("last_" + n) for n in (
             "on", "rden", "norm", "ot", "otc", "x1", "bn", "mv", "ln", "r", "t2n", "t2", "t2c", "f", "res"))

        def max_head(s):
            return s if s < NB else None

        def exp_head(s):
            return s - LAG if 0 <= s - LAG < NB else None

        def group(s, first):
            g, r = divmod(s - first, GH)
            return g if r == 0 and 0 <= g < NGRP else None

        def mt_group(s):
            return group(s, TURN_MAX)

        def nm_group(v):
            return group(v, GH)

        def av_group(s):
            return group(s, LAG + GH + 1)

        ON, OT, X1, NORM2, T2, FFN = 1, 3, 5, 6, 8, 10

        def tail(s, at):
            b, r = divmod(s - at - (LAG + NH + 1), NH)
            return b if r == 0 and 0 <= b < B - 1 else None

        LAST = NB + LAG + 1
        STEPS = LAST - NH + FFN + 1
        L = B - 1
        W2_STEP = LAG + NH + 4

        block = ctx.enter_context(nc.Block())

        @block.sync
        def _(sp):
            def store(b):
                sp.wait_ge(res_ok, b + 1)
                sp.dma_start(out_v[b], res[:, b, :]).then_inc(stored, 16)

            sp.dma_start(xs[:, 0, :], x_v[0]).then_inc(x_in[0], 16)
            sp.dma_start(wqkv_n[:, :, :], wqkv.rearrange("(a p) c -> p a c", p=P)).then_inc(wqkv_in, 16)
            sp.dma_start(xs[:, 1, :], x_v[1]).then_inc(x_in[1], 16)
            sp.dma_start(xs[:, 2, :], x_v[2]).then_inc(x_in[2], 16)
            sp.dma_start(xs[:, 3, :], x_v[3]).then_inc(x_in[3], 16)
            with nc.allow_non_contiguous_dma(reason="small vectors, one element per partition"):
                for part in (1, 0):
                    sp.dma_start(bqk[:, part:part + 1], bqkv.rearrange("(h p d a) -> p d h a", h=NH, p=3, a=1)[part]).then_inc(bqk_in, 16)
            sp.dma_start(wproj_n[:, :], wproj).then_inc(wproj_in, 16)
            sp.dma_start(wffn_n[:, :], wffn).then_inc(wffn_in, 16)
            sp.dma_start(qidx_i[:, :], qidx).then_inc(nf4_in, 16)
            sp.dma_start(scale_s[:, :], scales.rearrange("(o j) -> o j", o=P)).then_inc(nf4_in, 16)

            def stack(b, blocks):
                for i in blocks:
                    parts, sem_, value = ((slice(KHI, QHI + 1, 2), hi_ok, 2 * b + 2), (slice(KLO, QHI + 1), lo_ok, 2 * b + 1),
                                          (slice(KHI, QLO + 1, 3), lo_ok, 2 * b + 2), (slice(KLO, QLO + 1, 2), lo_ok, 2 * b + 2))[i]
                    sp.wait_ge(sem_, value)
                    sp.dma_start(stk[i * D:(i + 1) * D, b, :, :, :].bitcast(F32), hl[:, b, parts, :].bitcast(F32)).then_inc(stk_in[b], 16)

            for b in range(B - 1):
                stack(b, range(TERMS))
            for g in range(NGRP):
                b, h0 = g // NG, GH * (g % NG)
                sp.wait_ge(mt_ok, g + 1)
                sp.dma_start(stk[SROWS:SROWS + MROWS, b, h0:h0 + GH, Q, :].bitcast(F32), mt[:, g % 2, :].bitcast(F32)).then_inc(m_in[g % 2], 16)
                if g < 2:
                    stack(B - 1, range(2 * g, 2 * g + 2))
                if g == NGRP - 2:
                    store(0)
            for b in range(1, B - 1):
                store(b)
            for t in range(NT):
                sp.wait_ge(last_res, t + 1)
                sp.dma_start(out_v[L][:, t * P:(t + 1) * P], res[:, L, t * P:(t + 1) * P]).then_inc(stored, 16)
            sp.wait_ge(stored, 16 * (B - 1 + NT))

        @block.gpsimd
        def _(pool):
            pool.memset(ident[:, :], 0.0).then_inc(ident_zero, 1)
            pool.wait_ge(ident_zero, 1)
            pool.affine_select(out=ident[:, :], in_=ident[:, :], compare_op=ALU.not_equal, fill=1.0, base=0,
                               pattern=[[-1, P]], channel_multiplier=1).then_inc(ident_ok, 1)

            def fill(b, part, value, n):
                if n:
                    pool.wait_ge(fill_pool, n)
                pool.memset(stk[SROWS:P, b, :, part, :].bitcast(F32), value).then_inc(fill_pool, 1)

            pool.wait_ge(ident_ok, 1)
            fill(0, Q, 0.0, 0)
            pool.wait_ge(fill_pool, 1)
            pool.memset(vp[:, :, :, :, D:32].rearrange("p b t h d -> p (b t h) d"), 1.0).then_inc(vones_ok, 1)
            with nc.allow_non_contiguous_dma(reason="small vectors, one element per partition"):
                pool.dma_start(bvcol[:, :], bqkv.rearrange("(h p d a) -> p h d a", h=NH, p=3, a=1)[2]).then_inc(bv_in, 16)
                pool.dma_start(bpcol[:, :], col(bproj)).then_inc(bproj_in, 16)
            pool.wait_ge(vones_ok, 1)
            for b in (1, 2):
                fill(b, K, 1.0, 2 * b - 1)
                fill(b, Q, 0.0, 2 * b)
            pool.wait_ge(fill_pool, 5)
            pool.wait_ge(nf4_in, 32)
            pool.tensor_copy(qidx_f[:, :], qidx_i[:, :]).then_inc(nf4_step, 1)
            pool.wait_ge(nf4_step, 1)
            for k, value in enumerate(NF4):
                pool.tensor_scalar(pick[:, k, :], qidx_f[:, :], float(k), value, ALU.is_equal, ALU.mult).then_inc(nf4_step, 1)
            n, half = 1 + len(NF4), len(NF4) // 2
            while half:
                pool.wait_ge(nf4_step, n)
                pool.tensor_tensor(pick[:, 0:half, :], pick[:, 0:half, :], pick[:, half:2 * half, :], ALU.add).then_inc(nf4_step, 1)
                n, half = n + 1, half // 2
            pool.wait_ge(nf4_step, n)
            pool.tensor_tensor(lora_s[:, :, :], pick[:, 0, :].rearrange("o (j k) -> o j k", k=NF4_BLOCK),
                               scale_s[:, :].unsqueeze(2).to_broadcast([P, C // NF4_BLOCK, NF4_BLOCK]),
                               ALU.mult).then_inc(lora_ok, 1)

        @block.scalar
        def _(act):
            act.preload_act_table_set("natural_log_exp_and_others")
            with nc.allow_non_contiguous_dma(reason="small vectors, one element per partition"):
                act.dma_start(gcol[:, :], col(gamma)).then_inc(affine_in, 16)
                act.dma_start(bcol[:, :], col(beta)).then_inc(affine_in, 16)

            def fill(b, part, which):
                act.activation(stk[SROWS:P, b, :, part, :],
                               const[SROWS:P, which:which + 1].unsqueeze(2).to_broadcast([P - SROWS, NH, T]),
                               ACT.Copy).then_inc(fill_act, 1)

            act.wait_ge(const_ok, 2)
            fill(B - 1, K, 1)
            act.wait_ge(eps_ok, 2)

            def norm1_rstd(b):
                act.wait_ge(mv1, NT * (b + 1))
                act.activation(lnv[:, 0, b, :], mv[:, 0, b, :, 1], ACT.Ln, bias=eps1[:, 0:1], scale=1.0 + EPS_ATTN).then_inc(ln1, 1)
                act.wait_ge(ln1, b + 1)
                act.activation(rstd[:, 0, b, :], lnv[:, 0, b, :], ACT.Exp, scale=-0.5).then_inc(r1, 1)

            def affine(b):
                act.wait_ge(pe_tc, b + 1)
                if b == 0:
                    act.wait_ge(affine_in, 32)
                act.activation(tc[:, b, :], front(b)[:, T:2 * T], ACT.Identity, bias=bcol[:, 0:1],
                               scale=gcol[:, 0:1]).then_inc(tc_ok, 1)

            def split_hi(b):
                act.wait_ge(pe_qk, b + 1)
                if b == 0:
                    act.wait_ge(bqk_in, 32)
                act.activation(hl[:, b, KHI, :], qk_bank(b)[:, 0:T], ACT.Identity, bias=bqk[:, 1:2]).then_inc(hi_ok, 1)
                act.activation(hl[:, b, QHI, :], qk_bank(b)[:, T:2 * T], ACT.Identity, bias=bqk[:, 0:1]).then_inc(hi_ok, 1)

            def keep_v(b):
                act.wait_ge(pe_v, b + 1)
                if b == 0:
                    act.wait_ge(vones_ok, 1)
                act.activation(vp[:, b, :, :, 0:D].rearrange("p t h d -> p (t h) d"),
                               front(b)[:, 0:NT * C].rearrange("p (x d) -> p x d", d=D), ACT.Copy).then_inc(v_ok, 1)

            norm1_rstd(0)
            norm1_rstd(1)
            affine(0)
            norm1_rstd(2)
            affine(1)
            split_hi(0)
            norm1_rstd(3)
            affine(2)
            split_hi(1)
            act.wait_ge(pe_wx, 1)
            act.activation(wx_t[:, :, :].rearrange("c a o -> c (a o)"), TB[:, 0:2 * C], ACT.Copy).then_inc(wx_ok, 1)
            affine(3)
            keep_v(0)
            split_hi(2)
            act.wait_ge(pe_bpv, 1)
            act.wait_ge(bproj_in, 16)
            act.activation(bpv[:, :], TB[:, 0:1], ACT.Identity, bias=bpcol[:, 0:1]).then_inc(bpv_ok, 1)
            keep_v(1)
            split_hi(3)
            keep_v(2)
            keep_v(3)
            act.wait_ge(bpv_ok, 1)
            for b in range(B):
                act.wait_ge(x_in[b], 16)
                act.activation(xb[:, b, :], xs[:, b, :], ACT.Identity, bias=bpv[:, 0:1]).then_inc(xb_ok, 1)

            def keep_output(s):
                g = av_group(s)
                if g is not None and s < DVE_FROM:
                    b, gi = divmod(g, NG)
                    act.wait_ge(pe_av, g + 1)
                    if b >= 2 and gi == 0:
                        act.wait_ge(pe_on, b - 1)
                    act.activation(os_[:, b % 2, gi, :], OB[:, gi, :], ACT.Copy).then_inc(os_ok, 1)

            def keep_ot(s):
                b = tail(s, OT)
                if b is not None and s < DVE_FROM:
                    act.wait_ge(pe_ot, b + 1)
                    if b >= 2:
                        act.wait_ge(pe_f, b - 1)
                    act.activation(ot[:, b % 2, :], TA[:, 0:T], ACT.Copy).then_inc(ot_ok, 1)

            def keep_t2(s):
                b = tail(s, T2)
                if b is not None and s < DVE_FROM:
                    act.wait_ge(pe_t2, b + 1)
                    if b >= 2:
                        act.wait_ge(pe_f, b - 1)
                    act.activation(t2c[:, b % 2, :], TB[:, 0:T], ACT.Copy).then_inc(t2c_ok, 1)

            for s in range(STEPS):
                g = mt_group(s)
                if g is not None:
                    act.wait_ge(pe_mt, g + 1)
                    if g >= 2:
                        act.wait_ge(m_in[g % 2], 16 * (g // 2))
                    act.activation(mt[:, g % 2, :], TA[0:MROWS * GH, 0:T], ACT.Copy).then_inc(mt_ok, 1)
                    if g == 0:
                        fill(B - 1, Q, 0)
                v = exp_head(s)
                if v is not None:
                    act.wait_ge(pe_s, v + 1)
                    if v >= NE:
                        act.wait_ge(pe_av, (v - NE) // GH + 1)
                    act.activation(ex[:, v % NE, :, :].rearrange("p t q -> p (t q)"), exp_bank(v)[0], ACT.Exp,
                                   scale=float(D) ** -0.5).then_inc(ex_ok, 1)
                b = tail(s, NORM2)
                if b is not None:
                    act.wait_ge(mv2, NT * (b + 1))
                    act.activation(lnv[:, 1, b, :], mv[:, 1, b, :, 1], ACT.Ln, bias=eps2[:, 0:1]).then_inc(ln2, 1)
                    act.wait_ge(ln2, b + 1)
                    act.activation(rstd[:, 1, b, :], lnv[:, 1, b, :], ACT.Exp, scale=-0.5).then_inc(r2, 1)
                keep_output(s)
                keep_ot(s)
                keep_t2(s)

            for t in range(NT):
                act.wait_ge(last_ot, t + 1)
                if t == 0:
                    act.wait_ge(pe_f, L - 1)
                act.activation(ot[:, L % 2, t * P:(t + 1) * P], LAST_O[t][:, 0:P], ACT.Copy).then_inc(last_otc, 1)
            for t in range(NT):
                act.wait_ge(last_mv, t + 1)
                act.activation(lnv[:, 1, L, t:t + 1], mv[:, 1, L, t, 1:2], ACT.Ln, bias=eps2[:, 0:1]).then_inc(last_ln, 1)
                act.wait_ge(last_ln, t + 1)
                act.activation(rstd[:, 1, L, t:t + 1], lnv[:, 1, L, t:t + 1], ACT.Exp, scale=-0.5).then_inc(last_r, 1)
            for t in range(NT):
                act.wait_ge(last_t2, t + 1)
                act.activation(t2c[:, L % 2, t * P:(t + 1) * P], LAST_T2[t][:, 0:P], ACT.Copy).then_inc(last_t2c, 1)

        @block.vector
        def _(dve):
            dve.memset(eps1[:, :], EPS_ATTN * EPS_CHANNEL).then_inc(eps_ok, 1)
            dve.memset(eps2[:, :], EPS_FFN).then_inc(eps_ok, 1)

            dve.memset(const[:, 0:1], 0.0).then_inc(const_ok, 1)
            dve.memset(const[:, 1:2], 1.0).then_inc(const_ok, 1)
            dve.memset(stk[SROWS:P, 0, :, K, :].bitcast(F32), 1.0).then_inc(fill_dve, 1)

            def stats(which, b, src, bn, mvs):
                for t in range(NT):
                    dve.bn_stats(st6[:, which, b, t, :], src[:, t * C:(t + 1) * C]).then_inc(bn, 1)
                for t in range(NT):
                    dve.wait_ge(bn, NT * b + t + 1)
                    dve.bn_aggr(mv[:, which, b, t, :], st6[:, which, b, t, :]).then_inc(mvs, 1)

            def normalize(which, b, dst, src, r, done):
                dve.wait_ge(r, b + 1)
                for t in range(NT):
                    dve.tensor_scalar(dst[:, t, :], src[:, t * C:(t + 1) * C], mv[:, which, b, t, 0:1],
                                      rstd[:, which, b, t:t + 1], ALU.subtract, ALU.mult).then_inc(done, 1)

            def norm1_stats(b):
                dve.wait_ge(pe_xt, b + 1)
                stats(0, b, front(b), bn1, mv1)

            def norm1_apply(b):
                normalize(0, b, tn[:, b, :, :], front(b), r1, tn_ok)

            def split_lo(b):
                dve.wait_ge(hi_ok, 2 * b + 2)
                for i, (hi, lo) in enumerate(((KHI, KLO), (QHI, QLO))):
                    dve.scalar_tensor_tensor(out=hl[:, b, lo, :], in0=qk_bank(b)[:, i * T:(i + 1) * T],
                                             scalar=bqk[:, 1 - i:2 - i], in1=hl[:, b, hi, :].bitcast(F32),
                                             op0=ALU.add, op1=ALU.subtract).then_inc(lo_ok, 1)

            def maxima(s):
                v = max_head(s)
                if v is not None:
                    g = v // GH
                    dve.wait_ge(pe_max, v + 1)
                    if g >= 2 and v % GH == 0:
                        dve.wait_ge(nml_ok, g - 1)
                    dve.tensor_reduce(mx[:, g % 2, :, v % GH], SM[:, v % NM, :].rearrange("p (t k) -> p t k", t=NT),
                                      AX_X, ALU.max).then_inc(max_ok, 1)
                g = nm_group(s)
                if g is not None:
                    dve.wait_ge(max_ok, GH * (g + 1))
                    if g >= 2:
                        dve.wait_ge(pe_mt, g - 1)
                    dve.tensor_scalar(nm[:, g % 2, :, 0, :], mx[:, g % 2, :, :], -1.0, None, ALU.mult).then_inc(nmh_ok, 1)
                    dve.wait_ge(nmh_ok, g + 1)
                    dve.scalar_tensor_tensor(out=nm[:, g % 2, :, 1, :], in0=mx[:, g % 2, :, :], scalar=-1.0,
                                             in1=nm[:, g % 2, :, 0, :].bitcast(F32),
                                             op0=ALU.mult, op1=ALU.subtract).then_inc(nml_ok, 1)

            norm1_stats(0)
            dve.wait_ge(pe_w, 1)
            wt = TB[:, 0:3 * C].rearrange("c (h p d) -> c p d h", h=NH, p=3)
            dve.tensor_copy(wqk_t[:, :, :, :], wt[:, 0:2]).then_inc(w_ok, 1)
            norm1_stats(1)
            norm1_apply(0)
            dve.tensor_copy(wv_t[:, :, :], TB[:, 0:3 * C].rearrange("c (h p d) -> c p h d", h=NH, p=3)[:, 2]).then_inc(w_ok, 1)
            norm1_stats(2)
            norm1_apply(1)
            norm1_stats(3)
            norm1_apply(2)
            split_lo(0)
            norm1_apply(3)
            split_lo(1)
            split_lo(2)
            for s in range(EARLY):
                maxima(s)
            split_lo(3)

            def keep_output(s):
                g = av_group(s)
                if g is not None and s >= DVE_FROM:
                    b, gi = divmod(g, NG)
                    dve.wait_ge(pe_av, g + 1)
                    if b >= 2 and gi == 0:
                        dve.wait_ge(pe_on, b - 1)
                    dve.tensor_copy(os_[:, b % 2, gi, :], OB[:, gi, :]).then_inc(os_ok, 1)

            def keep_ot(s):
                b = tail(s, OT)
                if b is not None and s >= DVE_FROM:
                    dve.wait_ge(pe_ot, b + 1)
                    if b >= 2:
                        dve.wait_ge(pe_f, b - 1)
                    dve.tensor_copy(ot[:, b % 2, :], TA[:, 0:T]).then_inc(ot_ok, 1)

            def keep_t2(s):
                b = tail(s, T2)
                if b is not None and s >= DVE_FROM:
                    dve.wait_ge(pe_t2, b + 1)
                    if b >= 2:
                        dve.wait_ge(pe_f, b - 1)
                    dve.tensor_copy(t2c[:, b % 2, :], TB[:, 0:T]).then_inc(t2c_ok, 1)

            def result(b):
                dve.wait_ge(pe_f, b + 1)
                dve.wait_ge(xb_ok, b + 1)
                dve.tensor_tensor(res[:, b, :], TB[:, 0:T], xb[:, b, :], ALU.add).then_inc(res_ok, 1)

            for s in range(STEPS):
                if s >= EARLY:
                    maxima(s)
                if s == W2_STEP:
                    dve.wait_ge(pe_w2, 1)
                    dve.tensor_copy(w2_t[:, :], TB[:, 0:C]).then_inc(w2_ok, 1)
                keep_output(s)
                keep_ot(s)
                keep_t2(s)
                b = tail(s, FFN)
                if b is not None and b < L - 1:
                    result(b)
                b = tail(s, ON)
                if b is not None:
                    o = TA[:, :].rearrange("p (x e) -> p x e", e=32)
                    den = rden[:, b % 2, :, :].rearrange("p t h -> p (t h)")
                    dve.wait_ge(pe_on, b + 1)
                    dve.reciprocal(den, o[:, :, D]).then_inc(rden_ok, 1)
                    dve.wait_ge(rden_ok, b + 1)
                    dve.tensor_tensor(on[:, b % 2, :, :, :].rearrange("p t h d -> p (t h) d"), o[:, :, 0:D],
                                      den.unsqueeze(2).to_broadcast([P, NT * NH, D]), ALU.mult).then_inc(on_ok, 1)
                b = tail(s, X1)
                if b is not None:
                    dve.wait_ge(pe_x1, b + 1)
                    stats(1, b, TB, bn2, mv2)
                b = tail(s, NORM2)
                if b is not None:
                    normalize(1, b, t2n[:, b % 2, :, :], TB, r2, t2n_ok)

            for t in range(NT):
                o = LAST_O[t][:, 0:NG * P].rearrange("p (h e) -> p h e", e=32)
                dve.wait_ge(last_on, t + 1)
                dve.reciprocal(rden[:, L % 2, t, :], o[:, :, D]).then_inc(last_rden, 1)
                dve.wait_ge(last_rden, t + 1)
                dve.tensor_tensor(on[:, L % 2, t, :, :], o[:, :, 0:D],
                                  rden[:, L % 2, t, :].unsqueeze(2).to_broadcast([P, NH, D]), ALU.mult).then_inc(last_norm, 1)
            result(L - 1)
            for t in range(NT):
                dve.wait_ge(last_x1, t + 1)
                dve.bn_stats(st6[:, 1, L, t, :], LAST_X1[t][:, 0:C]).then_inc(last_bn, 1)
                dve.wait_ge(last_bn, t + 1)
                dve.bn_aggr(mv[:, 1, L, t, :], st6[:, 1, L, t, :]).then_inc(last_mv, 1)
            for t in range(NT):
                dve.wait_ge(last_r, t + 1)
                dve.tensor_scalar(t2n[:, L % 2, t, :], LAST_X1[t][:, 0:C], mv[:, 1, L, t, 0:1],
                                  rstd[:, 1, L, t:t + 1], ALU.subtract, ALU.mult).then_inc(last_t2n, 1)
            for t in range(NT):
                dve.wait_ge(last_f, t + 1)
                dve.wait_ge(xb_ok, B)
                dve.tensor_tensor(res[:, L, t * P:(t + 1) * P], LAST_F[t][:, 0:P], xb[:, L, t * P:(t + 1) * P],
                                  ALU.add).then_inc(last_res, 1)

        @block.tensor
        def _(pe):
            free = {}

            def take(bank, sem_, value):
                if bank.name in free:
                    pe.wait_ge(*free[bank.name])
                free[bank.name] = (sem_, value)

            def turn(dst, src):
                return pe.transpose(dst, src, ident[:, :])

            def x_turn(b):
                pe.wait_ge(x_in[b], 16)
                for t in range(NT):
                    last = turn(front(b)[:, t * C:(t + 1) * C], xs[:, b, t * P:(t + 1) * P])
                last.then_inc(pe_xt, 1)

            def t_turn(b):
                pe.wait_ge(tn_ok, NT * (b + 1))
                for t in range(NT):
                    last = turn(front(b)[:, T + t * P:T + (t + 1) * P], tn[:, b, t, :])
                last.then_inc(pe_tc, 1)

            def project(b):
                pe.wait_ge(tc_ok, b + 1)
                if b == 0:
                    pe.wait_ge(w_ok, 2)
                if b == NM:
                    take(TB, lo_ok, 2 * B)
                for i, part in enumerate((1, 0)):
                    if i and b + 1 < B:
                        t_turn(b + 1)
                    last = pe.matmul(qk_bank(b)[:, i * T:(i + 1) * T],
                                     wqk_t[:, part, :, :].rearrange("c d h -> c (d h)"), tc[:, b, :],
                                     start=True, stop=True)
                last.then_inc(pe_qk, 1)

            def values_of(b):
                if b == B - 1:
                    take(TA, v_ok, B)
                for t in range(NT):
                    last = pe.matmul(front(b)[:, t * C:(t + 1) * C], tc[:, b, t * P:(t + 1) * P],
                                     wv_t[:, :, :].rearrange("c h d -> c (h d)"), start=True, stop=True)
                last.then_inc(pe_v, 1)

            def keep_warm(n, dst):
                for _ in range(n):
                    turn(dst, ident[:, :])

            def max_scores(v):
                b, h = divmod(v, NH)
                if v < NM:
                    pe.wait_ge(lo_ok, 2 * (v + 1))
                else:
                    pe.wait_ge(max_ok, v - NM + 1)
                if h == 0:
                    pe.wait_ge(stk_in[b], 16 * TERMS)
                    if b == 0:
                        pe.wait_ge(fill_dve, 1)
                        pe.wait_ge(fill_pool, 1)
                    elif b < B - 1:
                        pe.wait_ge(fill_pool, 2 * b + 1)
                    else:
                        pe.wait_ge(fill_act, 2)
                for t in range(NT):
                    last = pe.matmul(SM[:, v % NM, t * T:(t + 1) * T], stk[:, b, h, Q, t * P:(t + 1) * P],
                                     stk[:, b, h, K, :], start=True, stop=True)
                last.then_inc(pe_max, 1)

            pe.wait_ge(ident_ok, 1)
            keep_warm(9, SM[:, 2, 0:P])
            x_turn(0)
            pe.wait_ge(wqkv_in, 16)
            take(TB, w_ok, 2)
            for a in range(3):
                last = turn(TB[:, a * C:(a + 1) * C], wqkv_n[:, a, :])
            last.then_inc(pe_w, 1)
            x_turn(1)
            keep_warm(3, SM[:, 2, 0:P])
            x_turn(2)
            t_turn(0)
            keep_warm(1, SM[:, 2, 0:P])
            x_turn(3)
            project(0)
            values_of(0)
            project(1)
            pe.wait_ge(wproj_in, 16)
            pe.wait_ge(wffn_in, 16)
            take(TB, wx_ok, 1)
            turn(TB[:, 0:C], wproj_n[:, :])
            turn(TB[:, C:2 * C], wffn_n[:, :]).then_inc(pe_wx, 1)
            project(2)
            values_of(1)
            pe.wait_ge(wx_ok, 1)
            pe.wait_ge(bv_in, 16)
            take(TB, bpv_ok, 1)
            pe.matmul(TB[:, 0:1], wproj_t, bvcol[:, 0:1], start=True, stop=True).then_inc(pe_bpv, 1)
            project(3)
            values_of(2)
            for v in range(EARLY):
                max_scores(v)
            values_of(3)

            def exp_scores(v):
                b, h = divmod(v, NH)
                bank, before = exp_bank(v)
                if before is not None:
                    pe.wait_ge(ex_ok, before + 1)
                elif v < NX:
                    pe.wait_ge(v_ok, v + 1)
                else:
                    pe.wait_ge(max_ok, NB)
                if v % GH == 0:
                    g = v // GH
                    pe.wait_ge(m_in[g % 2], 16 * (g // 2 + 1))
                for t in range(NT):
                    last = pe.matmul(bank[:, t * T:(t + 1) * T], stk[:, b, h, K, t * P:(t + 1) * P],
                                     stk[:, b, h, Q, :], start=True, stop=True)
                last.then_inc(pe_s, 1)

            def values(g):
                b, gi = divmod(g, NG)
                pe.wait_ge(ex_ok, GH * (g + 1))
                if g == 0:
                    pe.wait_ge(v_ok, B)
                if g:
                    pe.wait_ge(os_ok, g)
                for t in range(NT):
                    for i in range(GH):
                        last = pe.matmul(OB[32 * i:32 * i + 32, gi, :], vp[:, b, t, GH * gi + i, :],
                                         ex[:, (GH * g + i) % NE, t, :], start=(t == 0), stop=(t == NT - 1))
                last.then_inc(pe_av, 1)

            for s in range(STEPS):
                g = mt_group(s)
                if g is not None:
                    pe.wait_ge(nml_ok, g + 1)
                    take(TA, mt_ok, g + 1)
                    for t in range(NT):
                        last = turn(TA[0:MROWS * GH, t * P:(t + 1) * P],
                                    nm[:, g % 2, t, :, :].rearrange("p s h -> p (s h)").bitcast(F32))
                    last.then_inc(pe_mt, 1)
                if s >= EARLY and max_head(s) is not None:
                    max_scores(max_head(s))
                if s < LAG:
                    if s == 0:
                        pe.wait_ge(v_ok, NX)
                    keep_warm(1, SE[:, 1, 0:P])
                if exp_head(s) is not None:
                    exp_scores(exp_head(s))
                if av_group(s) is not None:
                    values(av_group(s))
                if s == W2_STEP:
                    pe.wait_ge(lora_ok, 1)
                    take(TB, w2_ok, 1)
                    pe.matmul(TB[:, 0:C], lora_s[:, :, :].rearrange("o j k -> o (j k)"), wffn_t,
                              start=True, stop=True).then_inc(pe_w2, 1)
                b = tail(s, FFN)
                if b is not None:
                    pe.wait_ge(t2c_ok, b + 1)
                    if b == 0:
                        pe.wait_ge(w2_ok, 1)
                    take(TB, res_ok, b + 1)
                    pe.matmul(TB[:, 0:T], w2_t[:, :], t2c[:, b % 2, :], start=True, stop=False)
                    pe.matmul(TB[:, 0:T], wproj_t, ot[:, b % 2, :], start=False, stop=True).then_inc(pe_f, 1)
                b = tail(s, ON)
                if b is not None:
                    pe.wait_ge(os_ok, NG * (b + 1))
                    take(TA, on_ok, b + 1)
                    for t in range(NT):
                        for gi in range(NG):
                            last = turn(TA[:, (t * NG + gi) * P:(t * NG + gi + 1) * P],
                                        os_[:, b % 2, gi, t * P:(t + 1) * P])
                    last.then_inc(pe_on, 1)
                b = tail(s, OT)
                if b is not None:
                    pe.wait_ge(on_ok, b + 1)
                    take(TA, ot_ok, b + 1)
                    for t in range(NT):
                        last = turn(TA[:, t * P:(t + 1) * P], on[:, b % 2, t, :, :].rearrange("p h d -> p (h d)"))
                    last.then_inc(pe_ot, 1)
                b = tail(s, X1)
                if b is not None:
                    pe.wait_ge(ot_ok, b + 1)
                    pe.wait_ge(xb_ok, b + 1)
                    take(TB, t2n_ok, NT * (b + 1))
                    for t in range(NT):
                        pe.matmul(TB[:, t * C:(t + 1) * C], xb[:, b, t * P:(t + 1) * P], ident[:, :],
                                  is_transpose=True, start=True, stop=False)
                        last = pe.matmul(TB[:, t * C:(t + 1) * C], ot[:, b % 2, t * P:(t + 1) * P], wproj_t,
                                         start=False, stop=True)
                    last.then_inc(pe_x1, 1)
                b = tail(s, T2)
                if b is not None:
                    pe.wait_ge(t2n_ok, NT * (b + 1))
                    take(TB, t2c_ok, b + 1)
                    for t in range(NT):
                        last = turn(TB[:, t * P:(t + 1) * P], t2n[:, b % 2, t, :])
                    last.then_inc(pe_t2, 1)
                if s == LAST + ON:
                    pe.wait_ge(os_ok, NGRP)
                    take(TA, last_norm, 1)
                    for t in range(NT):
                        for gi in range(NG):
                            last = turn(LAST_O[t][:, gi * P:(gi + 1) * P], os_[:, L % 2, gi, t * P:(t + 1) * P])
                        last.then_inc(last_on, 1)

            pe.wait_ge(xb_ok, B)
            for t in range(NT):
                pe.matmul(LAST_X1[t][:, 0:C], xb[:, L, t * P:(t + 1) * P], ident[:, :],
                          is_transpose=True, start=True, stop=False)
            for t in range(NT):
                pe.wait_ge(last_norm, t + 1)
                turn(LAST_O[t][:, 0:P], on[:, L % 2, t, :, :].rearrange("p h d -> p (h d)")).then_inc(last_ot, 1)
            keep_warm(4, LAST_T2[0][:, 0:P])
            for t in range(NT):
                pe.wait_ge(last_otc, t + 1)
                pe.matmul(LAST_X1[t][:, 0:C], ot[:, L % 2, t * P:(t + 1) * P], wproj_t,
                          start=False, stop=True).then_inc(last_x1, 1)
            take(TB, last_res, 1)
            for t in range(NT):
                pe.matmul(LAST_F[t][:, 0:P], wproj_t, ot[:, L % 2, t * P:(t + 1) * P], start=True, stop=False)
            keep_warm(6, LAST_T2[0][:, 0:P])
            for t in range(NT):
                pe.wait_ge(last_t2n, t + 1)
                turn(LAST_T2[t][:, 0:P], t2n[:, L % 2, t, :]).then_inc(last_t2, 1)
            for t in range(NT):
                pe.wait_ge(last_t2c, t + 1)
                pe.matmul(LAST_F[t][:, 0:P], w2_t[:, :], t2c[:, L % 2, t * P:(t + 1) * P],
                          start=False, stop=True).then_inc(last_f, 1)


_INS = ['x', 'L0_conv_gamma', 'L0_conv_beta', 'L0_conv_Wqkv', 'L0_conv_bqkv', 'L0_conv_Wproj', 'L0_conv_bproj',
        'L0_ffn_qidx', 'L0_ffn_scales', 'L0_ffn_W']


def kernel(**inputs):
    import numpy as _np
    import concourse.bacc as _bacc
    from concourse import mybir as _mybir
    from concourse.bass_utils import run_bass_kernel_spmd as _run

    nc = _bacc.Bacc("TRN2", target_bir_lowering=False, num_devices=1)
    arrays, args = {}, []
    for name in _INS:
        a = _np.ascontiguousarray(inputs[name])
        arrays[f"in_{name}_dram"] = a
        args.append(nc.dram_tensor(f"in_{name}_dram", a.shape, _mybir.dt.from_np(a.dtype), kind="ExternalInput").ap())
    shape = inputs['x'].shape
    out = nc.dram_tensor("out_0_dram", shape, _mybir.dt.float32, kind="ExternalOutput").ap()
    metaformer_kernel(nc, *args, out)
    r = _run(nc, [arrays], core_ids=[0])
    return r.results[0]["out_0_dram"]
```
